# Optimizing a Trainium2 kernel written in Bass

```python
import numpy as np
import jax
import jax.numpy as jnp

def _softmax(x, axis=-1):
    return jax.nn.softmax(x, axis=axis)

def _gelu(x):
    return jax.nn.gelu(x, approximate=True)

def _silu(x):
    return jax.nn.silu(x)

def _sigmoid(x):
    return jax.nn.sigmoid(x)

def _layernorm(x, axis=-1, eps=1e-05):
    m = jnp.mean(x, axis=axis, keepdims=True)
    v = jnp.var(x, axis=axis, keepdims=True)
    return (x - m) / jnp.sqrt(v + eps)

def _scatter_add(tgt, idx, src, axis=0):
    return tgt.at[idx].add(src)

def _segment_sum(src, seg, n):
    return jax.ops.segment_sum(src, seg, n)
kernel_name = 'mk_flamingo_gated_d1_seqx_r8_372a4a'

def setup_inputs(seed: int=0):
    np.random.seed(seed)
    _w = jnp.asarray

    def _rec_inputs():
        import jax
        import jax.numpy as jnp
        _rk = jax.random.key(seed)
        x = 0.0003765 + 1 * jax.random.normal(jax.random.fold_in(_rk, 1), (16, 128, 256), jnp.float32)
        _lenS = 128 - jax.random.randint(jax.random.fold_in(_rk, 7), (16,), 0, max(1, 128 // 4) + 1, jnp.int32)
        _lenS2 = 128 - jax.random.randint(jax.random.fold_in(_rk, 8), (16,), 0, max(1, 128 // 4) + 1, jnp.int32)
        _ctx_2048P = jax.random.normal(jax.random.fold_in(_rk, 11), (16, 16, 256), jnp.float32)
        _ctx_2048c = jax.random.dirichlet(jax.random.fold_in(_rk, 511), 0.3 * jnp.ones((16,), jnp.float32), (16, 128))
        _ctx_2048t = jnp.einsum('bsk,bkd->bsd', _ctx_2048c, _ctx_2048P)
        _ctx_2048t = _ctx_2048t * jax.lax.rsqrt(jnp.mean(jnp.square(_ctx_2048t)) + 1e-12) * 0.953939
        ctx_2048 = -0.000292821 + 1.00034 * (_ctx_2048t + 0.3 * jax.random.normal(jax.random.fold_in(_rk, 611), (16, 128, 256), jnp.float32))
        _g = jax.random.normal(jax.random.fold_in(_rk, 9001), (2, 1), jnp.float32)
        _g = jnp.sign(_g) * jnp.maximum(jnp.abs(_g), 1.0) + (_g == 0) * 1.0
        g_xattn = _g[0]
        g_ffn = _g[1]
        return (x, ctx_2048, g_xattn, g_ffn)
    x, ctx_2048, g_xattn, g_ffn = _rec_inputs()

    def _L0_xattn_setup():
        import jax, jax.numpy as jnp
        import numpy as np
        key = jax.random.key(seed)
        k1, k2, k3, k4, k5 = jax.random.split(key, 5)
        B, D_MODEL, L = (2, 128, 256)
        HEAD_DIM = 8
        H = D_MODEL // HEAD_DIM
        return {'k': jax.random.normal(k1, (B, D_MODEL, L), dtype=jnp.float32), 'v': jax.random.normal(k2, (B, D_MODEL, L), dtype=jnp.float32), 'q': jax.random.normal(k3, (B, D_MODEL, L), dtype=jnp.float32), 'ssm_kernel': jax.random.normal(k4, (H, L), dtype=jnp.float32), 'D': jax.random.normal(k5, (H,), dtype=jnp.float32), 'head_dim': HEAD_DIM}
    _L0_xattn_all = _L0_xattn_setup()
    _L0_xattn_in = {k: v for k, v in _L0_xattn_all.items() if k in ('ssm_kernel', 'D')}
    del _L0_xattn_all

    def _L0_ffn_setup():
        import jax, jax.numpy as jnp
        import numpy as np
        TOP_K = 2
        NUM_EXPERTS = 8
        ROUTE_SCALE = 1.0
        key = jax.random.key(seed)
        ks = jax.random.split(key, 8)
        bs, slen, dim, hidden, E = (4, 128, 256, 128, NUM_EXPERTS)
        s = 0.02
        return {'x': jax.random.normal(ks[0], (bs, slen, dim), jnp.float32), 'gate_w': jax.random.normal(ks[1], (E, dim), jnp.float32) * s, 'w1': jax.random.normal(ks[2], (E, hidden, dim), jnp.float32) * s, 'w2': jax.random.normal(ks[3], (E, dim, hidden), jnp.float32) * s, 'w3': jax.random.normal(ks[4], (E, hidden, dim), jnp.float32) * s, 'ws1': jax.random.normal(ks[5], (hidden, dim), jnp.float32) * s, 'ws2': jax.random.normal(ks[6], (dim, hidden), jnp.float32) * s, 'ws3': jax.random.normal(ks[7], (hidden, dim), jnp.float32) * s}
    _L0_ffn_all = _L0_ffn_setup()
    _L0_ffn_in = {k: v for k, v in _L0_ffn_all.items() if k in ('gate_w', 'w1', 'w2', 'w3', 'ws1', 'ws2', 'ws3')}
    del _L0_ffn_all
    return {'x': x, 'ctx_2048': ctx_2048, 'g_xattn': g_xattn, 'g_ffn': g_ffn, 'L0_xattn_ssm_kernel': _L0_xattn_in['ssm_kernel'], 'L0_xattn_D': _L0_xattn_in['D'], 'L0_ffn_gate_w': _L0_ffn_in['gate_w'], 'L0_ffn_w1': _L0_ffn_in['w1'], 'L0_ffn_w2': _L0_ffn_in['w2'], 'L0_ffn_w3': _L0_ffn_in['w3'], 'L0_ffn_ws1': _L0_ffn_in['ws1'], 'L0_ffn_ws2': _L0_ffn_in['ws2'], 'L0_ffn_ws3': _L0_ffn_in['ws3']}

def reference(x, ctx_2048, g_xattn, g_ffn, L0_xattn_ssm_kernel, L0_xattn_D, L0_ffn_gate_w, L0_ffn_w1, L0_ffn_w2, L0_ffn_w3, L0_ffn_ws1, L0_ffn_ws2, L0_ffn_ws3):
    import jax
    import jax.numpy as jnp

    def _L0_xattn_ref(k, v, q, ssm_kernel, D, head_dim):
        import jax, jax.numpy as jnp
        import numpy as np
        B, HD, L = k.shape
        H = HD // head_dim
        fft_size = 2 * L
        k_ = k.reshape(B, H, head_dim, L)
        v_ = v.reshape(B, H, head_dim, L)
        q_ = q.reshape(B, H, head_dim, L)
        kv = jnp.einsum('bhil,bhjl->bijhl', k_, v_)
        kv_f = jnp.fft.rfft(kv, n=fft_size)
        kernel_f = jnp.fft.rfft(ssm_kernel, n=fft_size)
        y = jnp.fft.irfft(kv_f * kernel_f, n=fft_size)[..., :L]
        out = y + kv * D[None, None, None, :, None]
        out = jnp.einsum('bijhl,bhil->bjhl', out, q_)
        out = jnp.transpose(out, (0, 2, 1, 3)).reshape(B, H * head_dim, L)
        return out.astype(k.dtype)

    def _L0_ffn_ref(x, gate_w, w1, w2, w3, ws1, ws2, ws3):
        import jax, jax.numpy as jnp
        import numpy as np
        TOP_K = 2
        NUM_EXPERTS = 8
        ROUTE_SCALE = 1.0
        bs, slen, dim = x.shape
        xf = x.reshape(-1, dim)
        logits = (xf @ gate_w.T).astype(jnp.float32)
        scores = jax.nn.sigmoid(logits)
        top_scores, sel_idx = jax.lax.top_k(scores, TOP_K)
        top_scores = top_scores * ROUTE_SCALE
        routed = jnp.zeros_like(xf)
        for k in range(TOP_K):
            xs = xf * top_scores[:, k][:, None]
            h1 = jnp.einsum('td,ehd->teh', xs, w1)
            h3 = jnp.einsum('td,ehd->teh', xs, w3)
            h = jax.nn.silu(h1) * h3
            onehot = jax.nn.one_hot(sel_idx[:, k], NUM_EXPERTS, dtype=h.dtype)
            routed = routed + jnp.einsum('teh,te,edh->td', h, onehot, w2)
        shared = jax.nn.silu(xf @ ws1.T) * (xf @ ws3.T) @ ws2.T
        out = (shared + routed).reshape(bs, slen, dim)
        return out
    x = x + jnp.tanh(g_xattn[0]) * _L0_xattn_ref(ctx_2048, ctx_2048, _layernorm(x, axis=-1), L0_xattn_ssm_kernel, L0_xattn_D, 8)
    x = x + jnp.tanh(g_ffn[0]) * _L0_ffn_ref(_layernorm(x, axis=-1), L0_ffn_gate_w, L0_ffn_w1, L0_ffn_w2, L0_ffn_w3, L0_ffn_ws1, L0_ffn_ws2, L0_ffn_ws3)
    return x

_drawn_inputs = setup_inputs


def setup_inputs(seed=0):
    import zlib

    import numpy as np

    out = dict(_drawn_inputs(seed))
    spreads = {}
    factors = {'L0_ffn_gate_w': 8.0,
     'L0_ffn_w1': 8.0,
     'L0_ffn_w2': 8.0,
     'L0_ffn_w3': 8.0,
     'L0_ffn_ws1': 8.0,
     'L0_ffn_ws2': 8.0,
     'L0_ffn_ws3': 8.0}
    for name, (base, spread) in spreads.items():
        noise = np.random.default_rng([zlib.crc32(name.encode()), seed]).standard_normal(out[name].shape)
        drawn = base * np.exp(spread * noise) if base else spread * noise
        out[name] = jnp.asarray(drawn.astype(out[name].dtype))
    for name, factor in factors.items():
        out[name] = (out[name] * factor).astype(out[name].dtype)
    return out
```

```python
from contextlib import ExitStack

import concourse.bass as bass
from concourse import mybir

F32 = mybir.dt.float32
F32R = mybir.dt.float32r
ALU = mybir.AluOpType
ACT = mybir.ActivationFunctionType
AX = mybir.AxisListType

P = 128
B, L, H, HD = 16, 256, 16, 8
C = L // P
HALF = HD // 2
NG, GB = 2, B // 2
CB = C * GB
NR = 8
NE, HID = NR + 1, 128
TOPK = 2
EPS = 1e-5
KPAD = P - 1 + L
RING = 4
W13 = C * NE * 2 * HID
W2 = NE * L
NW = NG * H
WP = (W13 + W2) // NW
DCOLS = 2 * CB * HALF * HALF
OCOLS = CB * HALF * HALF
PAIRS = (NE + 1) // 2
TWO = 2 * PAIRS


def pair_experts(k):
    return range(2 * k, min(2 * k + 2, NE))


def build(nc, x, kt, kpad, d_skip, g_both, gate_w, w_all, kpad_d, out):
    with ExitStack() as ctx:
        def sb(name, shape, dt=F32, stack=ctx):
            return stack.enter_context(nc.sbuf_tensor(name, shape, dt))

        def psum(name):
            return ctx.enter_context(nc.psum_tensor(name, [P, 512], F32))

        def sem(name):
            return ctx.enter_context(nc.semaphore(name))

        xs = sb("xs", [P, B, L])
        toep = sb("toep", [P, RING, L])
        kv = sb("kv", [P, 2, DCOLS + OCOLS])
        wst = sb("wst", [P, RING, WP])
        wH = sb("wH", [P, W13 + W2], F32R)
        wL = sb("wL", [P, W13 + W2], F32R)
        gw = sb("gw", [P, C * NR])
        gwH = sb("gwH", [P, C * NR], F32R)
        gwL = sb("gwL", [P, C * NR], F32R)
        xn = sb("xn", [P, GB, L])
        stats = sb("stats", [P, B, 6])
        mv1 = sb("mv1", [P, GB, 2])
        mv2 = sb("mv2", [P, B, 2])
        std = sb("std", [P, B])
        rstd = sb("rstd", [P, B])
        kp = sb("kp", [H, KPAD])
        dsk = sb("dsk", [H, 1])
        gx = sb("gx", [P, 2])
        tg = sb("tg", [P, 2])
        ident = sb("ident", [P, P])
        epsc = sb("epsc", [P, 1])
        score = sb("score", [P, B, NR])
        before = sb("before", [P, NR, NR])
        rank = sb("rank", [P, GB, NR])
        gates = sb("gates", [P, B, NE])
        with ExitStack() as stage1:
            kT = sb("kT", [P, NG, H, 2 * CB * HALF], F32, stage1)
            qT = sb("qT", [P, NG, H, 2, C, GB * HALF], F32, stage1)
            z = sb("z", [P, 2, CB * HALF, P], F32, stage1)
        xTH = sb("xTH", [P, B, L], F32R)
        xTL = sb("xTL", [P, B, L], F32R)
        tH = sb("tH", [P, 2, L], F32R)
        tL = sb("tL", [P, 2, L], F32R)
        cgt = sb("cgt", [P, GB, NR, NR])
        ceq = sb("ceq", [P, GB, NR, NR])
        silu = sb("silu", [P, 2, 2, HID])
        hid = sb("hid", [P, 2, 2, HID])
        hTH = sb("hTH", [P, 2, 2 * P], F32R)
        hTL = sb("hTL", [P, 2, 2 * P], F32R)
        ob = sb("ob", [P, 2, L])

        yD = [psum(f"yD{i}") for i in range(2)]
        yO = [psum(f"yO{i}") for i in range(2)]
        att = [psum(f"att{i}") for i in range(2)]
        tp = [psum(f"tp{i}") for i in range(2)]
        up, hT = yD, yO
        lg = att
        yy = tp

        s_kt = [sem(f"s_kt{g}") for g in range(NG)]
        s_x = [sem(f"s_x{g}") for g in range(NG)]
        s_kp = sem("s_kp")
        s_small = sem("s_small")
        s_kpd = sem("s_kpd")
        s_kpd_stored = sem("s_kpd_stored")
        s_toep = [sem(f"s_toep{u}") for u in range(RING)]
        s_wst = [sem(f"s_wst{u}") for u in range(RING)]
        s_zero = sem("s_zero")
        s_const = sem("s_const")
        s_kv = sem("s_kv")
        s_conv = sem("s_conv")
        s_z = sem("s_z")
        s_isum = sem("s_isum")
        s_x2 = sem("s_x2")
        s_tg = sem("s_tg")
        s_st = sem("s_st")
        s_mv = sem("s_mv")
        s_std = sem("s_std")
        s_rstd = sem("s_rstd")
        s_xn = sem("s_xn")
        s_tp = sem("s_tp")
        s_qT = sem("s_qT")
        s_wH = sem("s_wH")
        s_wL = sem("s_wL")
        s_gw = sem("s_gw")
        s_xTH = sem("s_xTH")
        s_xTL = sem("s_xTL")
        s_lg = sem("s_lg")
        s_score = sem("s_score")
        s_rank = sem("s_rank")
        s_gates = sem("s_gates")
        s_tile = [sem(f"s_tile{p}") for p in range(2)]
        s_up = sem("s_up")
        s_silu = sem("s_silu")
        s_hid = sem("s_hid")
        s_hT = sem("s_hT")
        s_hTH = sem("s_hTH")
        s_hTL = sem("s_hTL")
        s_down = sem("s_down")
        s_ob = sem("s_ob")
        s_out = [sem(f"s_out{p}") for p in range(2)]

        block = ctx.enter_context(nc.Block())

        @block.sync
        def _(sp):
            sp.dma_start(kp[:, :], kpad).then_inc(s_kp, 16)
            sp.dma_start(dsk[:, :], d_skip).then_inc(s_kp, 16)
            sp.dma_start(kT[:, 0, :, :].rearrange("p h n -> p (h n)"), kt[:, 0, :]).then_inc(s_kt[0], 16)
            sp.dma_start(gx[:, :], g_both.to_broadcast([P, 2])).then_inc(s_small, 16)
            sp.dma_start(gw[:, :], gate_w).then_inc(s_small, 16)
            sp.wait_ge(s_kpd, 1)
            sp.dma_start(kpad_d, kp[:, :]).then_inc(s_kpd_stored, 16)
            sp.wait_ge(s_kpd_stored, 16)
            toep_rows = bass.AP(tensor=kpad_d.tensor, offset=0, ap=[[KPAD, H], [1, P], [1, L]])
            for g in range(NG):
                with sp.Fori(0, H // RING) as it:
                    for u in range(RING):
                        n = it * RING + (g * H + u)
                        sp.wait_ge(s_conv, n + 1)
                        sp.dma_start(toep[:, u, :], toep_rows[it * RING + u]).then_inc(s_toep[u], 16)
                        sp.wait_ge(s_wL, n + 1)
                        sp.dma_start(wst[:, u, :], w_all[:, n, :]).then_inc(s_wst[u], 16)
                if g == 0:
                    sp.dma_start(kT[:, 1, :, :].rearrange("p h n -> p (h n)"), kt[:, 1, :]).then_inc(s_kt[1], 16)

            def load_tile(t, p):
                sp.dma_start(tH[:, p, :].bitcast(F32), xTH[:, t, :].bitcast(F32)).then_inc(s_tile[p], 16)
                sp.dma_start(tL[:, p, :].bitcast(F32), xTL[:, t, :].bitcast(F32)).then_inc(s_tile[p], 16)

            for p in range(2):
                sp.wait_ge(s_xTL, 1)
                load_tile(p, p)
            sp.wait_ge(s_xTL, B // 2)
            with sp.Fori(1, B // 2) as i:
                for p in range(2):
                    sp.wait_ge(s_up, i * TWO + (p - 1) * PAIRS)
                    load_tile(i * 2 + p, p)
                for p in range(2):
                    sp.wait_ge(s_ob, i * 2 + (p - 1))
                    sp.dma_start(out[:, i * 2 + (p - 2), :], ob[:, p, :]).then_inc(s_out[p], 16)
            for p in range(2):
                sp.wait_ge(s_ob, B - 1 + p)
                sp.dma_start(out[:, B - 2 + p, :], ob[:, p, :]).then_inc(s_out[p], 16)
            for p in range(2):
                sp.wait_ge(s_out[p], 16 * (B // 2))

        @block.gpsimd
        def _(pool):
            pool.memset(ident[:, :], 0.0).then_inc(s_zero, 1)
            pool.memset(before[:, :, :], 0.0).then_inc(s_zero, 1)
            pool.memset(epsc[:, :], EPS).then_inc(s_const, 1)
            pool.memset(gates[:, :, NR:NE], 1.0).then_inc(s_const, 1)
            pool.wait_ge(s_zero, 2)
            pool.affine_select(out=ident[:, :], in_=ident[:, :], compare_op=ALU.not_equal, fill=1.0,
                               base=0, pattern=[[-1, P]], channel_multiplier=1).then_inc(s_const, 1)
            pool.affine_select(out=before[:, :, :], in_=before[:, :, :], compare_op=ALU.is_ge, fill=1.0,
                               base=0, pattern=[[-1, NR], [1, NR]], channel_multiplier=0).then_inc(s_const, 1)
            for g in range(NG):
                pool.wait_ge(s_kt[g], 16)
                with pool.Fori(0, H // 2) as it:
                    for u in range(2):
                        k_h = kT[:, g, it * 2 + u, :].rearrange("p (s i) -> p s i", i=HALF)
                        kd = kv[:, u, 0:DCOLS].rearrange("p (s i j) -> p s i j", i=HALF, j=HALF)
                        ko = kv[:, u, DCOLS:].rearrange("p (s i j) -> p s i j", i=HALF, j=HALF)
                        full, off = [P, 2 * CB, HALF, HALF], [P, CB, HALF, HALF]
                        pool.wait_ge(s_conv, it * 2 + (g * H + u + RING - 1))
                        pool.tensor_tensor(kd, k_h.unsqueeze(3).to_broadcast(full),
                                           k_h.unsqueeze(2).to_broadcast(full), ALU.mult)
                        pool.tensor_tensor(ko, k_h[:, 0:CB, :].unsqueeze(3).to_broadcast(off),
                                           k_h[:, CB:2 * CB, :].unsqueeze(2).to_broadcast(off),
                                           ALU.mult).then_inc(s_kv, 1)

        @block.tensor
        def _(pe):
            def transpose_rows(m):
                pe.wait_ge(s_xn, 2 * m + 2)
                if 2 <= m < B // 2 + 2:
                    pe.wait_ge(s_qT, m - 1)
                if m >= B // 2 + 2:
                    pe.wait_ge(s_xTL, m - 1 - B // 2)
                for q in range(2):
                    for c in range(C):
                        mm = pe.transpose(tp[m % 2][:, q * L + c * P:q * L + (c + 1) * P],
                                          xn[:, (2 * m + q) % GB, c * P:(c + 1) * P], ident[:, :])
                mm.then_inc(s_tp, 1)

            def logits(t):
                pe.wait_ge(s_xTL, t // 2 + 1)
                o = lg[t // GB][:, t % GB * NR:(t % GB + 1) * NR]
                for c in range(C):
                    cols, w = slice(c * P, (c + 1) * P), slice(c * NR, (c + 1) * NR)
                    pe.matmul(o, xTH[:, t, cols], gwH[:, w], start=(c == 0), stop=False)
                    pe.matmul(o, xTH[:, t, cols], gwL[:, w], start=False, stop=False)
                    mm = pe.matmul(o, xTL[:, t, cols], gwH[:, w], start=False, stop=(c == C - 1))
                mm.then_inc(s_lg, 1)

            pe.sem_inc(s_conv, RING)
            pe.wait_ge(s_const, 4)
            for g in range(NG):
                for m in range(GB // 2):
                    transpose_rows(g * GB // 2 + m)
                with pe.Fori(0, H // RING) as it:
                    for u in range(RING):
                        n = it * RING + (g * H + u)
                        pe.wait_ge(s_toep[u], it * 16 + 16 * (g * H // RING + 1))
                        pe.wait_ge(s_kv, n + 1)
                        pe.wait_ge(s_z, n + 1)
                        A, BB, kvu = toep[:, u, 0:P], toep[:, u, P:L], kv[:, u % 2, :]
                        yd, yo = yD[u % 2][:, 0:DCOLS], yO[u % 2][:, 0:OCOLS]
                        kd, ko = kvu[:, 0:DCOLS], kvu[:, DCOLS:]
                        pe.matmul(yd, A, kd, start=True, stop=False)
                        pe.matmul(yo, A, ko, start=True, stop=False)
                        yd, kd = (v.rearrange("p (s c n) -> p s c n", s=2, c=C) for v in (yd, kd))
                        yo, ko = (v.rearrange("p (c n) -> p c n", c=C) for v in (yo, ko))
                        pe.matmul(yd[:, :, 1, :], BB, kd[:, :, 0, :], start=False, stop=True)
                        pe.matmul(yo[:, 1, :], BB, ko[:, 0, :], start=False, stop=True).then_inc(s_conv, 1)
                pe.wait_ge(s_z, H * (g + 1) + 2)
                for b in range(GB):
                    m = (g * GB + b) // 2
                    if b % 2 == 0 and m >= 2:
                        pe.wait_ge(s_x2, m - 1)
                    for c in range(C):
                        for i in range(HD):
                            mm = pe.matmul(att[m % 2][:, b % 2 * L + c * P:b % 2 * L + (c + 1) * P],
                                           z[:, i // HALF, (c * GB + b) * HALF + i % HALF, :],
                                           ident[:, :], is_transpose=True,
                                           start=(i == 0), stop=(i == HD - 1))
                    if b % 2:
                        mm.then_inc(s_isum, 1)

            pe.wait_ge(s_gw, 2)
            for m in range(B // 2 + 1):
                if m < B // 2:
                    transpose_rows(B // 2 + m)
                if m >= 1:
                    logits(2 * m - 2)
                    logits(2 * m - 1)

            def body(i, first, last=False):
                for j in range(TWO + (2 if last else 0)):
                    p, k = divmod(j, PAIRS)
                    if j < TWO:
                        if k == 0:
                            pe.wait_ge(s_tile[p], i * 32 + 32)
                        if not first or j >= 2:
                            pe.wait_ge(s_hid, i * TWO + (j - 1))
                        n = 2 * HID * len(pair_experts(k))
                        o = up[j % 2][:, 0:n]
                        for c in range(C):
                            cols, w0 = slice(c * P, (c + 1) * P), (c * NE + 2 * k) * 2 * HID
                            pe.matmul(o, tH[:, p, cols], wH[:, w0:w0 + n], start=(c == 0), stop=False)
                            pe.matmul(o, tH[:, p, cols], wL[:, w0:w0 + n], start=False, stop=False)
                            mm = pe.matmul(o, tL[:, p, cols], wH[:, w0:w0 + n], start=False, stop=(c == C - 1))
                        mm.then_inc(s_up, 1)
                    if (j >= 1 or not first) and j <= TWO:
                        k1 = (j - 1) % PAIRS
                        pe.wait_ge(s_hid, i * TWO + j)
                        if not first or j >= 3:
                            pe.wait_ge(s_hTL, i * TWO + (j - 2))
                        for q, _ in enumerate(pair_experts(k1)):
                            mm = pe.transpose(hT[(j - 1) % 2][:, q * P:(q + 1) * P],
                                              hid[:, (j - 1) % 2, q, :], ident[:, :])
                        mm.then_inc(s_hT, 1)
                    if j >= 2 or not first:
                        k2, p2 = (j - 2) % PAIRS, (j - 2) % TWO // PAIRS
                        pe.wait_ge(s_hTL, i * TWO + (j - 1))
                        if k2 == 0 and not (first and j - 2 < TWO):
                            pe.wait_ge(s_ob, i * 2 + (0 if j - 2 < 0 else p2 - 1))
                        o = yy[p2][:, 0:L]
                        for q, e in enumerate(pair_experts(k2)):
                            hh, w0 = slice(q * P, (q + 1) * P), W13 + e * L
                            pe.matmul(o, hTH[:, j % 2, hh], wH[:, w0:w0 + L], start=(e == 0), stop=False)
                            pe.matmul(o, hTH[:, j % 2, hh], wL[:, w0:w0 + L], start=False, stop=False)
                            mm = pe.matmul(o, hTL[:, j % 2, hh], wH[:, w0:w0 + L], start=False, stop=(e == NE - 1))
                        mm.then_inc(s_down, 1)

            pe.wait_ge(s_wL, NW + RING)
            body(0, first=True)
            with pe.Fori(1, B // 2 - 1) as i:
                body(i, first=False)
            body(B // 2 - 1, first=False, last=True)

        @block.scalar
        def _(act):
            for g in range(NG):
                act.dma_start(xs[:, g * GB:(g + 1) * GB, :], x[:, g * GB:(g + 1) * GB, :]).then_inc(s_x[g], 16)
            act.wait_ge(s_small, 32)
            act.wait_ge(s_const, 4)
            act.activation(tg[:, :], gx[:, :], ACT.Tanh).then_inc(s_tg, 1)
            for g in range(NG):
                act.wait_ge(s_mv, GB * (2 * g + 1))
                act.activation(std[:, 0:GB], mv1[:, :, 1], ACT.Sqrt, bias=epsc[:, :]).then_inc(s_std, 1)
                for b in range(GB):
                    n = g * GB + b
                    src = tp[n // 2 % 2][:, n % 2 * L:(n % 2 + 1) * L].rearrange("p (c s i) -> p s c i", c=C, i=HALF)
                    dst = qT[:, g, :, :, :, b * HALF:(b + 1) * HALF].rearrange("p h s c i -> p (h s) c i")
                    act.wait_ge(s_tp, n // 2 + 1)
                    mm = act.copy(dst, src)
                    if n % 2:
                        mm.then_inc(s_qT, 1)
                with act.Fori(0, H // RING) as it:
                    for u in range(RING):
                        n = it * RING + (g * H + u)
                        act.wait_ge(s_wst[u], it * 16 + 16 * (g * H // RING + 1))
                        act.copy(wH[:, bass.ds(n * WP, WP)], wst[:, u, :]).then_inc(s_wH, 1)
            act.wait_ge(s_mv, NG * 2 * GB)
            act.activation(std[:, :], mv2[:, :, 1], ACT.Sqrt, bias=epsc[:, :]).then_inc(s_std, 1)
            for m in range(B // 2):
                act.wait_ge(s_tp, B // 2 + m + 1)
                act.copy(xTH[:, 2 * m:2 * m + 2, :].rearrange("p t n -> p (t n)"), tp[m % 2][:, :]).then_inc(s_xTH, 1)
                if 2 * m % GB == GB - 2:
                    g = 2 * m // GB
                    act.wait_ge(s_lg, GB * (g + 1))
                    act.activation(score[:, g * GB:(g + 1) * GB, :].rearrange("p t e -> p (t e)"),
                                   lg[g][:, 0:GB * NR], ACT.Sigmoid).then_inc(s_score, 1)

            def body(i, first, last=False):
                for j in range(TWO + (1 if last else 0)):
                    p, k = divmod(j, PAIRS)
                    if j < TWO:
                        act.wait_ge(s_up, i * TWO + (j + 1))
                        if not first or j >= 2:
                            act.wait_ge(s_hid, i * TWO + (j - 1))
                        for q, e in enumerate(pair_experts(k)):
                            mm = act.activation(silu[:, j % 2, q, :], up[j % 2][:, q * 2 * HID:(q * 2 + 1) * HID],
                                                ACT.Silu, scale=gates[:, i * 2 + p, e:e + 1])
                        mm.then_inc(s_silu, 1)
                    if j >= 1 or not first:
                        n = P * len(pair_experts((j - 1) % PAIRS))
                        act.wait_ge(s_hT, i * TWO + j)
                        if not first or j >= 3:
                            act.wait_ge(s_down, i * TWO + (j - 2))
                        act.copy(hTH[:, (j - 1) % 2, 0:n], hT[(j - 1) % 2][:, 0:n]).then_inc(s_hTH, 1)

            act.wait_ge(s_gates, NG)
            body(0, first=True)
            with act.Fori(1, B // 2 - 1) as i:
                body(i, first=False)
            body(B // 2 - 1, first=False, last=True)

        @block.vector
        def _(dve):
            def normalise(n, src, mv, b):
                if n >= GB:
                    dve.wait_ge(s_tp, (n - GB) // 2 + 1)
                dve.tensor_scalar(xn[:, n % GB, :], src, mv[:, b, 0:1], rstd[:, b:b + 1],
                                  ALU.subtract, ALU.mult).then_inc(s_xn, 1)

            def rank_gates(g):
                sc = score[:, g * GB:(g + 1) * GB, :]
                shape = [P, GB, NR, NR]
                mine, other = sc.unsqueeze(3).to_broadcast(shape), sc.unsqueeze(2).to_broadcast(shape)
                n = 6 * g
                dve.wait_ge(s_score, g + 1)
                dve.tensor_tensor(cgt[:, :, :, :], other, mine, ALU.is_gt).then_inc(s_rank, 1)
                dve.tensor_tensor(ceq[:, :, :, :], other, mine, ALU.is_equal).then_inc(s_rank, 1)
                dve.wait_ge(s_rank, n + 2)
                ce = ceq[:, :, :, :].rearrange("p t e f -> p t (e f)")
                bf = before[:, :, :].rearrange("p e f -> p (e f)").unsqueeze(1).to_broadcast([P, GB, NR * NR])
                dve.tensor_tensor(ce, ce, bf, ALU.mult).then_inc(s_rank, 1)
                dve.wait_ge(s_rank, n + 3)
                dve.tensor_tensor(cgt[:, :, :, :], cgt[:, :, :, :], ceq[:, :, :, :], ALU.add).then_inc(s_rank, 1)
                dve.wait_ge(s_rank, n + 4)
                dve.tensor_reduce(rank[:, :, :], cgt[:, :, :, :], AX.X, ALU.add).then_inc(s_rank, 1)
                dve.wait_ge(s_rank, n + 5)
                dve.tensor_scalar(rank[:, :, :], rank[:, :, :], float(TOPK), None, ALU.is_lt).then_inc(s_rank, 1)
                dve.wait_ge(s_rank, n + 6)
                dve.tensor_tensor(gates[:, g * GB:(g + 1) * GB, 0:NR], sc, rank[:, :, :], ALU.mult).then_inc(s_gates, 1)

            dve.sem_inc(s_z, 2)
            dve.sem_inc(s_wL, RING)
            dve.wait_ge(s_kp, 32)
            dve.tensor_tensor(kp[:, P - 1:P], kp[:, P - 1:P], dsk[:, :], ALU.add).then_inc(s_kpd, 1)
            for g in range(NG):
                dve.wait_ge(s_x[g], 16)
                m = 2 * g * GB
                if g:
                    dve.wait_ge(s_mv, m)
                for b in range(GB):
                    dve.bn_stats(stats[:, b, :], xs[:, g * GB + b, :]).then_inc(s_st, 1)
                if g:
                    dve.wait_ge(s_xn, GB)
                for b in range(GB):
                    dve.wait_ge(s_st, m + b + 1)
                    dve.bn_aggr(mv1[:, b, :], stats[:, b, :]).then_inc(s_mv, 1)
                dve.wait_ge(s_std, g + 1)
                dve.reciprocal(rstd[:, 0:GB], std[:, 0:GB]).then_inc(s_rstd, 1)
                dve.wait_ge(s_rstd, g + 1)
                for b in range(GB):
                    normalise(g * GB + b, xs[:, g * GB + b, :], mv1, b)
                if g == 0:
                    dve.wait_ge(s_small, 32)
                    dve.tensor_copy(gwH[:, :], gw[:, :]).then_inc(s_gw, 1)
                    dve.wait_ge(s_gw, 1)
                    dve.tensor_tensor(gwL[:, :], gw[:, :], gwH[:, :].bitcast(F32), ALU.subtract).then_inc(s_gw, 1)
                dve.wait_ge(s_qT, GB // 2 * (g + 1))
                if g:
                    dve.wait_ge(s_isum, GB // 2 * g)
                with dve.Fori(0, H // RING) as it:
                    for u in range(RING):
                        n = it * RING + (g * H + u)
                        yd = yD[u % 2][:, 0:DCOLS].rearrange("p (s n j) -> p s n j", s=2, j=HALF)
                        yo = yO[u % 2][:, 0:OCOLS].rearrange("p (n j) -> p n j", j=HALF)
                        q_h = qT[:, g, it * RING + u, :, :, :].rearrange("p s c n -> p s (c n)")
                        zh = z[:, :, :, bass.ds((it * RING + u) * HD, HD)]
                        ni = CB * HALF
                        dve.wait_ge(s_conv, n + (1 + RING))
                        dve.tensor_tensor(zh[:, 0, :, :].rearrange("p n (s j) -> p s n j", s=2), yd,
                                          q_h.unsqueeze(3).to_broadcast([P, 2, ni, HALF]), ALU.mult)
                        dve.tensor_tensor(zh[:, 1, :, HALF:], yo,
                                          q_h[:, 0, :].unsqueeze(2).to_broadcast([P, ni, HALF]), ALU.mult)
                        q_j = q_h[:, 1, :].rearrange("p (n j) -> p n j", j=HALF)
                        dve.tensor_tensor(zh[:, 1, :, 0:HALF].rearrange("p (n j) i -> p n i j", j=HALF),
                                          yo.rearrange("p (n i) j -> p n i j", i=HALF),
                                          q_j.unsqueeze(2).to_broadcast([P, CB, HALF, HALF]),
                                          ALU.mult).then_inc(s_z, 1)
                        dve.wait_ge(s_wH, n + 1)
                        w = bass.ds(n * WP, WP)
                        dve.tensor_tensor(wL[:, w], wst[:, u, :], wH[:, w].bitcast(F32), ALU.subtract).then_inc(s_wL, 1)
                dve.wait_ge(s_tg, 1)
                m = (2 * g + 1) * GB
                for k in range(GB // 2 + 1):
                    j = g * GB // 2 + k
                    if k < GB // 2:
                        xp = xs[:, 2 * j:2 * j + 2, :].rearrange("p t n -> p (t n)")
                        dve.wait_ge(s_isum, j + 1)
                        dve.scalar_tensor_tensor(out=xp, in0=att[j % 2][:, :], scalar=tg[:, 0:1], in1=xp,
                                                 op0=ALU.mult, op1=ALU.add).then_inc(s_x2, 1)
                    if k >= 1:
                        dve.wait_ge(s_x2, j)
                        for b in (2 * k - 2, 2 * k - 1):
                            dve.bn_stats(stats[:, b, :], xs[:, g * GB + b, :]).then_inc(s_st, 1)
                        for b in (2 * k - 2, 2 * k - 1):
                            dve.wait_ge(s_st, m + b + 1)
                            dve.bn_aggr(mv2[:, g * GB + b, :], stats[:, b, :]).then_inc(s_mv, 1)
            dve.wait_ge(s_std, NG + 1)
            dve.reciprocal(rstd[:, :], std[:, :]).then_inc(s_rstd, 1)
            dve.wait_ge(s_rstd, NG + 1)
            lead = 2
            for m in range(B // 2 + lead):
                if m < B // 2:
                    for t in (2 * m, 2 * m + 1):
                        normalise(B + t, xs[:, t, :], mv2, t)
                if m >= lead:
                    r = m - lead
                    pair = slice(2 * r, 2 * r + 2)
                    dve.wait_ge(s_xTH, r + 1)
                    dve.tensor_tensor(xTL[:, pair, :].rearrange("p t n -> p (t n)"), tp[r % 2][:, :],
                                      xTH[:, pair, :].rearrange("p t n -> p (t n)").bitcast(F32),
                                      ALU.subtract).then_inc(s_xTL, 1)
                    if 2 * r % GB == GB - 2:
                        rank_gates(2 * r // GB)

            def finish_tile(t, p, i):
                dve.wait_ge(s_down, t * PAIRS + PAIRS)
                if i is not None:
                    dve.wait_ge(s_out[p], i * 16)
                dve.scalar_tensor_tensor(out=ob[:, p, :], in0=yy[p][:, 0:L], scalar=tg[:, 1:2],
                                         in1=xs[:, t, :], op0=ALU.mult, op1=ALU.add).then_inc(s_ob, 1)

            def body(i, first, last=False):
                for j in range(TWO + (1 if last else 0)):
                    p, k = divmod(j, PAIRS)
                    if j < TWO:
                        dve.wait_ge(s_silu, i * TWO + (j + 1))
                        if not first or j >= 2:
                            dve.wait_ge(s_hT, i * TWO + (j - 1))
                        for q, e in enumerate(pair_experts(k)):
                            mm = dve.scalar_tensor_tensor(
                                out=hid[:, j % 2, q, :], in0=up[j % 2][:, (q * 2 + 1) * HID:(q * 2 + 2) * HID],
                                scalar=gates[:, i * 2 + p, e:e + 1], in1=silu[:, j % 2, q, :],
                                op0=ALU.mult, op1=ALU.mult)
                        mm.then_inc(s_hid, 1)
                    if j >= 1 or not first:
                        n = P * len(pair_experts((j - 1) % PAIRS))
                        dve.wait_ge(s_hTH, i * TWO + j)
                        if not first or j >= 3:
                            dve.wait_ge(s_down, i * TWO + (j - 2))
                        dve.tensor_tensor(hTL[:, (j - 1) % 2, 0:n], hT[(j - 1) % 2][:, 0:n],
                                          hTH[:, (j - 1) % 2, 0:n].bitcast(F32), ALU.subtract).then_inc(s_hTL, 1)
                    if j == 2 and not first:
                        finish_tile(i * 2 - 1, 1, None if isinstance(i, int) and i == 1 else i - 1)
                    if j == PAIRS + 2:
                        finish_tile(i * 2, 0, None if first else i)

            body(0, first=True)
            with dve.Fori(1, B // 2 - 1) as i:
                body(i, first=False)
            body(B // 2 - 1, first=False, last=True)
            finish_tile(B - 1, 1, B // 2 - 1)


def kernel(x, ctx_2048, g_xattn, g_ffn, L0_xattn_ssm_kernel, L0_xattn_D, L0_ffn_gate_w,
           L0_ffn_w1, L0_ffn_w2, L0_ffn_w3, L0_ffn_ws1, L0_ffn_ws2, L0_ffn_ws3):
    import numpy as np
    import concourse.bacc as bacc
    from concourse.bass_utils import run_bass_kernel_spmd as run

    cont = np.ascontiguousarray
    a = [np.asarray(v) for v in (x, ctx_2048, g_xattn, g_ffn, L0_xattn_ssm_kernel, L0_xattn_D, L0_ffn_gate_w,
                                 L0_ffn_w1, L0_ffn_w2, L0_ffn_w3, L0_ffn_ws1, L0_ffn_ws2, L0_ffn_ws3)]
    x, cx, gxa, gff, ssm, dsk, gate, w1, w2, w3, ws1, ws2, ws3 = a
    kt = cx.reshape(NG, GB, H, 2, HALF, C, P)[..., ::-1].transpose(6, 0, 2, 3, 5, 1, 4)
    kpad = np.zeros((H, KPAD), ssm.dtype)
    kpad[:, P - 1:] = ssm
    up = np.stack([np.concatenate([w1, ws1[None]]), np.concatenate([w3, ws3[None]])], 1)
    up = up.reshape(NE, 2, HID, C, P).transpose(4, 3, 0, 1, 2).reshape(P, W13)
    down = np.concatenate([w2, ws2[None]]).transpose(2, 0, 1).reshape(P, W2)
    arrays = {
        "x": cont(x.transpose(1, 0, 2)),
        "kt": cont(kt).reshape(P, NG, H * 2 * CB * HALF),
        "kpad": kpad,
        "d_skip": cont(dsk.reshape(H, 1)),
        "g_both": cont(np.concatenate([gxa, gff]).reshape(1, 2)),
        "gate_w": cont(gate.reshape(NR, C, P).transpose(2, 1, 0)).reshape(P, C * NR),
        "w_all": cont(np.concatenate([up, down], 1)).reshape(P, NW, WP),
    }
    nc = bacc.Bacc("TRN2", target_bir_lowering=False, num_devices=1)
    ins = [nc.dram_tensor(f"in_{n}", v.shape, F32, kind="ExternalInput").ap() for n, v in arrays.items()]
    kpad_d = nc.dram_tensor("kpad_d", (H, KPAD), F32, kind="Internal").ap()
    out = nc.dram_tensor("out", (P, B, L), F32, kind="ExternalOutput").ap()
    build(nc, *ins, kpad_d, out)
    r = run(nc, [{f"in_{n}": v for n, v in arrays.items()}], core_ids=[0])
    return cont(r.results[0]["out"].transpose(1, 0, 2))
```

```python
from contextlib import ExitStack, nullcontext

import concourse.bass as bass
from concourse import mybir

F32 = mybir.dt.float32
F32R = mybir.dt.float32r
BF16 = mybir.dt.bfloat16
I32 = mybir.dt.int32
U32 = mybir.dt.uint32
ALU = mybir.AluOpType
ACT = mybir.ActivationFunctionType
AX = mybir.AxisListType

P = 128
B, L, H, HD = 16, 256, 16, 8
C = L // P
HALF = HD // 2
NG, GB = 2, B // 2
CB = C * GB
NR = 8
NE, HID = NR + 1, 128
TOPK = 2
EPS = 1e-5
KPAD = P - 1 + L
RING = 4
WE = C * 2 * HID + L
NPIECE = H
WP = NE * WE // NPIECE
DCOLS = 2 * CB * HALF * HALF
OCOLS = CB * HALF * HALF
GP = GB // 2
NT = 24
SP = NT // 2
NS = NG * SP
SHARED = 0
K_ID, K_UP, K_BEF, K_THR, K_TILE = 0, P, 2 * P, 2 * P + NR * NR, 2 * P + NR * NR + NR
NK = K_TILE + NT


def build(nc, x, kt, kpad, d_skip, g_both, gate_w, w_all, consts, kpad_d, xg_d, y_d, out):
    with ExitStack() as ctx:
        def sb(name, shape, dt=F32, stack=ctx):
            return stack.enter_context(nc.sbuf_tensor(name, shape, dt))

        def psum(name):
            return ctx.enter_context(nc.psum_tensor(name, [P, 512], F32))

        def sem(name):
            return ctx.enter_context(nc.semaphore(name))

        xs = sb("xs", [P, B, L])
        toep = sb("toep", [P, RING, L])
        kv = sb("kv", [P, 2, DCOLS + OCOLS])
        wH = sb("wH", [P, NE * WE], F32R)
        wL = sb("wL", [P, NE * WE], F32R)
        gw = sb("gw", [P, C * NR])
        gwH = sb("gwH", [P, C * NR], F32R)
        gwL = sb("gwL", [P, C * NR], F32R)
        xq = sb("xq", [P, 4, L])
        xn = sb("xn", [P, B, L])
        early = xn[:, GB:, :].rearrange("p t n -> p (t n)")
        wst = early[:, 0:2 * WP].rearrange("p (u n) -> p u n", u=2)
        kp = early[0:H, 2 * WP:2 * WP + KPAD]
        dsk = early[0:H, 2 * WP + KPAD:2 * WP + KPAD + 1]
        stats = sb("stats", [P, 2, GB, 6])
        mv1 = sb("mv1", [P, GB, 2])
        mv2 = sb("mv2", [P, GB, 2])
        std = sb("std", [P, 2, GB])
        rstd = sb("rstd", [P, 2, GB])
        gx = sb("gx", [P, 2])
        tg = sb("tg", [P, 2])
        const = sb("const", [P, NK])
        ident = const[:, K_ID:K_ID + P]
        before = const[:, K_BEF:K_BEF + NR * NR]
        thr = const[:, K_THR:K_THR + NR]
        tile_no = const[:, K_TILE:K_TILE + NT]
        upper = sb("upper", [P, P], BF16)
        ones = sb("ones", [P, P], BF16)
        epsc = sb("epsc", [P, 1])
        tH = sb("tH", [P, 2, 2 * L], F32R)
        tL = sb("tL", [P, 2, 2 * L], F32R)
        silu = sb("silu", [P, 2, 2, HID])
        hid = sb("hid", [P, 2, 2, HID])
        hTH = sb("hTH", [P, 2, 2 * P], F32R)
        hTL = sb("hTL", [P, 2, 2 * P], F32R)
        logit = sb("logit", [P, GB, NR])
        score = sb("score", [P, GB, NR])
        cgt, ceq = (xq[:, 2 * v:2 * v + 2, :].rearrange("p a (b f) -> p (a b) f", f=NR) for v in range(2))
        rank = sb("rank", [P, GB * NR])
        sel = sb("sel", [P, TOPK, GB * NR])
        both = sb("both", [P, GB * NR], BF16)
        pick = sb("pick", [P, TOPK, GB * NR])
        gates = sb("gates", [P, NG, TOPK, GB])
        cnt = sb("cnt", [P, (GB + 1) * NR])
        ntile = sb("ntile", [P, NR])
        base = sb("base", [P, NR])
        ends = sb("ends", [P, NR])
        slot = sb("slot", [P, GB * NR])
        slotf = sb("slotf", [P, TOPK * GB])
        etf = sb("etf", [P, NT])
        etile = sb("etile", [P, NG, NT], I32)
        idx = sb("idx", [P, NG, TOPK, GB], U32)
        sx = sb("sx", [P, 4, L])
        with ExitStack() as stage1:
            kT = sb("kT", [P, H, 2 * CB * HALF], F32, stage1)
            qT = sb("qT", [P, H, 2, C, GB * HALF], F32, stage1)
            z = sb("z", [P, 2, CB * HALF, P], F32, stage1)
        got = sb("got", [P, B, TOPK, L])
        xrow = sb("xrow", [P, RING, 2, L])
        yrow = sb("yrow", [P, RING, 2, L])

        yD = [psum(f"yD{i}") for i in range(2)]
        yO = [psum(f"yO{i}") for i in range(2)]
        att = [psum(f"att{i}") for i in range(2)]
        tp = [psum(f"tp{i}") for i in range(2)]
        up, hT, yy = yD, yO, att
        ROUTE = 2 * P

        s_kt = [sem(f"s_kt{g}") for g in range(NG)]
        s_x = [sem(f"s_x{g}") for g in range(NG)]
        s_kp = sem("s_kp")
        s_small = sem("s_small")
        s_kpd = sem("s_kpd")
        s_kpd_stored = sem("s_kpd_stored")
        s_toep = [sem(f"s_toep{u}") for u in range(RING)]
        s_wst = [sem(f"s_wst{u}") for u in range(2)]
        s_zero = sem("s_zero")
        s_const = sem("s_const")
        s_upper = sem("s_upper")
        s_kv = sem("s_kv")
        s_conv = sem("s_conv")
        s_z = sem("s_z")
        s_isum = sem("s_isum")
        s_x2 = sem("s_x2")
        s_tg = sem("s_tg")
        s_st = [sem(f"s_st{i}") for i in range(2)]
        s_mv = [sem(f"s_mv{i}") for i in range(2)]
        s_std = sem("s_std")
        s_rstd = sem("s_rstd")
        s_xq = sem("s_xq")
        s_xn = sem("s_xn")
        s_kept = sem("s_kept")
        s_tp = sem("s_tp")
        s_qT = sem("s_qT")
        s_wH = sem("s_wH")
        s_wL = sem("s_wL")
        s_gw = sem("s_gw")
        s_tH = sem("s_tH")
        s_tL = sem("s_tL")
        s_up = sem("s_up")
        s_logit = sem("s_logit")
        s_lg = sem("s_lg")
        s_score = sem("s_score")
        s_rank = sem("s_rank")
        s_both = sem("s_both")
        s_gates = sem("s_gates")
        s_cnt = sem("s_cnt")
        s_cnt_read = sem("s_cnt_read")
        s_slot = sem("s_slot")
        s_etile = sem("s_etile")
        s_idx = sem("s_idx")
        s_xg_zero = sem("s_xg_zero")
        s_sx = sem("s_sx")
        s_sent = [sem(f"s_sent{r}") for r in range(4)]
        s_xrow = [sem(f"s_xrow{r}") for r in range(RING)]
        s_silu = sem("s_silu")
        s_hid = sem("s_hid")
        s_hT = sem("s_hT")
        s_hTH = sem("s_hTH")
        s_hTL = sem("s_hTL")
        s_down = sem("s_down")
        s_shared = sem("s_shared")
        s_yrow = sem("s_yrow")
        s_stored = [sem(f"s_stored{r}") for r in range(RING)]
        s_got = [sem(f"s_got{t}") for t in range(B)]
        s_sum = sem("s_sum")
        s_fin = sem("s_fin")
        s_out = sem("s_out")

        block = ctx.enter_context(nc.Block())

        A_SLOT, T_SLOT, N_SLOT = 2 * NG * GP, NG * GP, GP
        half = SP // RING
        NJ = NS + GP

        def piece(g, it, u):
            return it * 2 + (g * H // 2 + u // 2)

        @block.sync
        def _(sp):
            sp.dma_start(kp[:, :], kpad).then_inc(s_kp, 16)
            sp.dma_start(dsk[:, :], d_skip).then_inc(s_kp, 16)
            sp.dma_start(kT[:, :, :].rearrange("p h n -> p (h n)"), kt[:, 0, :]).then_inc(s_kt[0], 16)
            sp.dma_start(const[:, :], consts).then_inc(s_small, 16)
            sp.dma_start(gx[:, :], g_both.to_broadcast([P, 2])).then_inc(s_small, 16)
            sp.dma_start(gw[:, :], gate_w).then_inc(s_small, 16)
            sp.wait_ge(s_kpd, 1)
            sp.dma_start(kpad_d, kp[:, :]).then_inc(s_kpd_stored, 16)
            sp.wait_ge(s_kpd_stored, 16)
            toep_rows = bass.AP(tensor=kpad_d.tensor, offset=0, ap=[[KPAD, H], [1, P], [1, L]])
            for g in range(NG):
                with sp.Fori(0, H // RING) as it:
                    for u in range(RING):
                        h = it * RING + u
                        sp.wait_ge(s_conv, h + (g * H + 1))
                        sp.dma_start(toep[:, u, :], toep_rows[h]).then_inc(s_toep[u], 16)
                        if u % 2 == 0:
                            n = piece(g, it, u)
                            sp.wait_ge(s_wL, n + 1)
                            sp.dma_start(wst[:, u // 2, :], w_all[:, n, :]).then_inc(s_wst[u // 2], 16)
                if g == 0:
                    sp.wait_ge(s_kv, H)
                    sp.dma_start(kT[:, :, :].rearrange("p h n -> p (h n)"), kt[:, 1, :]).then_inc(s_kt[1], 16)

            def load(i, u, g):
                rows = xg_d[g].rearrange("(j t p) d -> j p t d", t=2, p=P)
                sp.wait_ge(s_tp, i * RING + (A_SLOT + u + 1 - RING))
                sp.dma_start(xrow[:, u, :, :], rows[i * RING + (u - g * SP)]).then_inc(s_xrow[u], 16)

            def store(i, u, g):
                rows = y_d[g].rearrange("(j t p) d -> j p t d", t=2, p=P)
                sp.wait_ge(s_yrow, i * RING + (u + 1 - 2 * RING))
                sp.dma_start(rows[i * RING + (u - 2 * RING - g * SP)], yrow[:, u, :, :]).then_inc(s_stored[u], 16)

            for first, end, g_load, g_store in ((0, 2, 0, None), (2, half, 0, 0), (half, half + 2, 1, 0),
                                                (half + 2, 2 * half, 1, 1), (2 * half, 2 * half + 2, None, 1)):
                if first in (0, half):
                    for r in range(4):
                        sp.wait_ge(s_sent[r], 16 * (g_load + 1) * (GB * TOPK // 4))
                with sp.Fori(first, end) as i:
                    for u in range(RING):
                        if g_load is not None:
                            load(i, u, g_load)
                        if g_store is not None:
                            store(i, u, g_store)
            with sp.Fori(0, B) as t:
                sp.wait_ge(s_fin, t + 1)
                sp.dma_start(out[:, t, :], xs[:, t, :]).then_inc(s_out, 16)
            sp.wait_ge(s_out, 16 * B)

        @block.gpsimd
        def _(pool):
            pool.memset(ones[:, :], 1.0).then_inc(s_const, 1)
            pool.memset(epsc[:, :], EPS).then_inc(s_const, 1)
            pool.memset(sx[:, :, :], 0.0).then_inc(s_const, 1)
            for g in range(NG):
                pool.wait_ge(s_kt[g], 16)
                with pool.Fori(0, H // 2) as it:
                    for u in range(2):
                        k_h = kT[:, it * 2 + u, :].rearrange("p (s i) -> p s i", i=HALF)
                        kd = kv[:, u, 0:DCOLS].rearrange("p (s i j) -> p s i j", i=HALF, j=HALF)
                        ko = kv[:, u, DCOLS:].rearrange("p (s i j) -> p s i j", i=HALF, j=HALF)
                        full, off = [P, 2 * CB, HALF, HALF], [P, CB, HALF, HALF]
                        pool.wait_ge(s_conv, it * 2 + (g * H + u + RING - 1))
                        pool.tensor_tensor(kd, k_h.unsqueeze(3).to_broadcast(full),
                                           k_h.unsqueeze(2).to_broadcast(full), ALU.mult)
                        pool.tensor_tensor(ko, k_h[:, 0:CB, :].unsqueeze(3).to_broadcast(off),
                                           k_h[:, CB:2 * CB, :].unsqueeze(2).to_broadcast(off),
                                           ALU.mult).then_inc(s_kv, 1)
            pool.wait_ge(s_xg_zero, 16 * NG)
            for g in range(NG):
                pool.wait_ge(s_gates, g + 1)
                pool.wait_ge(s_kept, GP)
                pool.wait_ge(s_idx, g + 1)
                for t in range(GB):
                    for k in range(TOPK):
                        n = g * GB * TOPK + t * TOPK + k
                        r = n % 4
                        if n >= 4:
                            pool.wait_ge(s_sent[r], 16 * (n // 4))
                        pool.tensor_scalar(sx[:, r, :], xn[:, g * GB + t, :], gates[:, g, k, t:t + 1], 1.0,
                                           ALU.mult, ALU.mult).then_inc(s_sx, 1)
                        pool.wait_ge(s_sx, n + 1)
                        pool.indirect_dma_start(
                            out=xg_d[g], out_offset=bass.IndirectOffsetOnAxis(ap=idx[:, g, k, t:t + 1], axis=0),
                            in_=sx[:, r, :], in_offset=None).then_inc(s_sent[r], 16)
            for g in range(NG):
                for r in range(RING):
                    pool.wait_ge(s_stored[r], 16 * (g + 1) * SP // RING)
                for t in range(GB):
                    for k in range(TOPK):
                        pool.indirect_dma_start(
                            out=got[:, g * GB + t, k, :], out_offset=None, in_=y_d[g],
                            in_offset=bass.IndirectOffsetOnAxis(ap=idx[:, g, k, t:t + 1], axis=0),
                        ).then_inc(s_got[g * GB + t], 16)

        @block.tensor
        def _(pe):
            def stage_a(bank, src):
                for q in range(2):
                    for c in range(C):
                        mm = pe.transpose(bank[:, q * L + c * P:q * L + (c + 1) * P],
                                          src(q)[:, c * P:(c + 1) * P], ident)
                mm.then_inc(s_tp, 1)

            def three(o, aH, aL, w, start, stop):
                pe.matmul(o, aH, wH[:, w], start=start, stop=False)
                pe.matmul(o, aH, wL[:, w], start=False, stop=False)
                return pe.matmul(o, aL, wH[:, w], start=False, stop=stop)

            def stage_b(bank, p, experts):
                for q, e in enumerate(experts):
                    for c in range(C):
                        cols = slice(q * L + c * P, q * L + (c + 1) * P)
                        mm = three(bank[:, q * L:(q + 1) * L], tH[:, p, cols], tL[:, p, cols],
                                   bass.ds(e + c * 2 * HID, 2 * HID), c == 0, c == C - 1)
                mm.then_inc(s_up, 1)

            def stage_c(bank, p):
                for q in range(2):
                    mm = pe.transpose(bank[:, q * P:(q + 1) * P], hid[:, p, q, :], ident)
                mm.then_inc(s_hT, 1)

            def stage_d(bank, p, experts):
                for q, e in enumerate(experts):
                    cols = slice(q * P, (q + 1) * P)
                    mm = three(bank[:, q * L:(q + 1) * L], hTH[:, p, cols], hTL[:, p, cols],
                               bass.ds(e + C * 2 * HID, L), True, True)
                mm.then_inc(s_down, 1)

            def logits(bank, p):
                for q in range(2):
                    o = bank[:, ROUTE + q * NR:ROUTE + (q + 1) * NR]
                    for c in range(C):
                        cols, w = slice(q * L + c * P, q * L + (c + 1) * P), slice(c * NR, (c + 1) * NR)
                        pe.matmul(o, tH[:, p, cols], gwH[:, w], start=(c == 0), stop=False)
                        pe.matmul(o, tH[:, p, cols], gwL[:, w], start=False, stop=False)
                        mm = pe.matmul(o, tL[:, p, cols], gwH[:, w], start=False, stop=(c == C - 1))
                return mm

            def q_pair(g, m):
                pe.wait_ge(s_xq, g * GB + 2 * m + 2)
                if g * GP + m >= 2:
                    pe.wait_ge(s_qT, g * GP + m - 1)
                stage_a(tp[m % 2], lambda q: xq[:, (2 * m + q) % 4, :])

            def token_stage(it, u):
                start = isinstance(it, int)
                if u == 0:
                    pe.wait_ge(s_xn, it * 2 + 2)
                    pe.wait_ge(s_qT, NG * GP) if start else pe.wait_ge(s_tL, it)
                    stage_a(tp[0], lambda q: xq[:, q, :])
                elif u == 1:
                    pe.wait_ge(s_tL, it + 1)
                    if start:
                        pe.wait_ge(s_x2, GP)
                        pe.wait_ge(s_gw, 2)
                        pe.wait_ge(s_wL, 2 + 2)
                    else:
                        pe.wait_ge(s_hid, it)
                        pe.wait_ge(s_hTL, it)
                    logits(att[0], 0)
                    stage_b(tp[1], 0, [SHARED] * 2)
                elif u == 2:
                    pe.wait_ge(s_hid, it + 1)
                    stage_c(att[0], 0)
                else:
                    pe.wait_ge(s_hTL, it + 1)
                    if not start:
                        pe.wait_ge(s_shared, it)
                    stage_d(att[1], 0, [SHARED] * 2)

            def tokens_logits():
                for j in range(GP + 1):
                    n = GP + j
                    if j < GP:
                        pe.wait_ge(s_xn, 2 * n + 2)
                        if j == 1:
                            pe.wait_ge(s_hid, GP)
                        if j >= 2:
                            pe.wait_ge(s_tL, n - 1)
                        stage_a(tp[j % 2], lambda q: xn[:, 2 * n + q, :])
                    if j >= 1:
                        pe.wait_ge(s_tL, n)
                        if j >= 3:
                            pe.wait_ge(s_logit, n - 2)
                        logits(hT[(j - 1) % 2], (j - 1) % 2).then_inc(s_lg, 1)

            def count(g, p):
                pe.wait_ge(s_both, g + 1)
                place = hT[p][:, ROUTE:ROUTE + GB * NR]
                total = hT[p][:, ROUTE + GB * NR:ROUTE + (GB + 1) * NR]
                pe.matmul(place, upper[:, :], both[:, :], start=True, stop=False)
                for t in range(GB - 1):
                    later = GB - 1 - t
                    row = both[:, t * NR:(t + 1) * NR].unsqueeze(1).to_broadcast([P, later, NR])
                    pe.matmul(place[:, (t + 1) * NR:].rearrange("p (t e) -> p t e", e=NR), ones[:, :], row,
                              start=False, stop=(t == GB - 2))
                for t in range(GB):
                    mm = pe.matmul(total, ones[:, :], both[:, t * NR:(t + 1) * NR], start=(t == 0),
                                   stop=(t == GB - 1))
                mm.then_inc(s_cnt, 1)

            def conv(g, it, u):
                n = it * RING + (g * H + u)
                pe.wait_ge(s_toep[u], it * 16 + 16 * (g * H // RING + 1))
                pe.wait_ge(s_kv, n + 1)
                pe.wait_ge(s_z, n + 1)
                A, BB, kvu = toep[:, u, 0:P], toep[:, u, P:L], kv[:, u % 2, :]
                yd, yo = yD[u % 2][:, 0:DCOLS], yO[u % 2][:, 0:OCOLS]
                kd, ko = kvu[:, 0:DCOLS], kvu[:, DCOLS:]
                pe.matmul(yd, A, kd, start=True, stop=False)
                pe.matmul(yo, A, ko, start=True, stop=False)
                yd, kd = (v.rearrange("p (s c n) -> p s c n", s=2, c=C) for v in (yd, kd))
                yo, ko = (v.rearrange("p (c n) -> p c n", c=C) for v in (yo, ko))
                pe.matmul(yd[:, :, 1, :], BB, kd[:, :, 0, :], start=False, stop=True)
                pe.matmul(yo[:, 1, :], BB, ko[:, 0, :], start=False, stop=True).then_inc(s_conv, 1)

            def isum(g, m):
                for q in range(2):
                    for c in range(C):
                        for i in range(HD):
                            mm = pe.matmul(att[m % 2][:, q * L + c * P:q * L + (c + 1) * P],
                                           z[:, i // HALF, (c * GB + 2 * m + q) * HALF + i % HALF, :],
                                           ident, is_transpose=True, start=(i == 0), stop=(i == HD - 1))
                mm.then_inc(s_isum, 1)

            pe.sem_inc(s_conv, RING)
            pe.wait_ge(s_small, 48)
            for m in range(GP):
                q_pair(0, m)
            with pe.Fori(0, H // RING) as it:
                for u in range(RING):
                    conv(0, it, u)
            pe.wait_ge(s_z, H + 2)
            for m in range(GP):
                if m >= 2:
                    pe.wait_ge(s_x2, m - 1)
                isum(0, m)
                q_pair(1, m)
            for first, end in ((0, 1), (1, H // RING)):
                with (nullcontext(0) if first == 0 else pe.Fori(first, end)) as it:
                    for u in range(RING):
                        conv(1, it, u)
                        token_stage(it, u)
            pe.wait_ge(s_z, NG * H + 2)
            for m in range(GP):
                if m < 2:
                    pe.wait_ge(*((s_hTL, s_shared)[m], GP))
                else:
                    pe.wait_ge(s_x2, GP + m - 1)
                isum(1, m)
                if m == 1:
                    count(0, 0)
            pe.wait_ge(s_cnt_read, 1)
            tokens_logits()

            def experts(i, first, end):
                n = 2 * (end - first)
                tiles = etile_flat[0:1, 2 * (RING * i + first):2 * (RING * i + end)] if isinstance(i, int) \
                    else etile_flat[0:1, bass.ds(i * (2 * RING) + 2 * first, n)]
                _, v = nc.values_load_multi_w_load_instructions(
                    tiles, engines=[mybir.EngineType.PE], min_val=0, max_val=(NR - 1) * WE,
                    skip_runtime_bounds_check_because="slots() clamps the tile's expert to the last one")
                return {first + k: [e + WE for e in v[2 * k:2 * k + 2]] for k in range(n // 2)}

            etile_flat = etile[:, :, :].rearrange("p g t -> p (g t)")

            def step(i, u, e, first=False, last=0):
                j, p = i * RING + u, u % 2
                tokens = isinstance(j, int) and j >= NS
                if last == 0:
                    if not tokens:
                        pe.wait_ge(s_xrow[u], i * 16 + 16)
                    pe.wait_ge(s_tL, j + (T_SLOT - 1))
                    stage_a(tp[p], lambda q: xn[:, GB + 2 * (j - NS) + q, :] if tokens else xrow[:, u, q, :])
                if last <= 1 and not (first and j < 1):
                    pe.wait_ge(s_tL, j + T_SLOT)
                    pe.wait_ge(s_hid, j + (N_SLOT - 2))
                    stage_b(up[1 - p], 1 - p, e[j - 1 if tokens else u - 1])
                if last <= 2 and not (first and j < 2):
                    pe.wait_ge(s_hid, j + (N_SLOT - 1))
                    pe.wait_ge(s_hTL, j + (N_SLOT - 3))
                    stage_c(hT[p], p)
                if not (first and j < 3):
                    pe.wait_ge(s_hTL, j + (N_SLOT - 2))
                    if tokens and j >= NS + 5:
                        pe.wait_ge(s_shared, j - 4 - NS + GP)
                    elif not (first and j < 5):
                        pe.wait_ge(s_yrow, j - 4)
                    stage_d(yy[1 - p], 1 - p, e[j - 3 if tokens else u - 3])

            pe.wait_ge(s_logit, NG * GP)
            e = experts(0, 0, 3)
            for u in range(RING):
                if u == 2:
                    count(1, 0)
                    pe.wait_ge(s_cnt_read, NG)
                step(0, u, e, first=True)
            e = experts(1, -3, 3)
            for u in range(RING):
                step(1, u, e, first=(u == 0))
            with pe.Fori(2, half) as i:
                e = experts(i, -3, 3)
                for u in range(RING):
                    step(i, u, e)
            pe.wait_ge(s_etile, 2)
            with pe.Fori(half, 2 * half) as i:
                e = experts(i, -3, 3)
                for u in range(RING):
                    step(i, u, e)
            e = {NS + k: v for k, v in experts(2 * half, -3, 0).items()}
            e.update({j: [SHARED] * 2 for j in range(NS, NJ)})
            for j in range(NS, NJ + 3):
                step(j // RING, j % RING, e, last=max(0, j - NJ + 1))

        @block.scalar
        def _(act):
            for g in range(NG):
                act.dma_start(xs[:, g * GB:(g + 1) * GB, :], x[:, g * GB:(g + 1) * GB, :]).then_inc(s_x[g], 16)
            act.wait_ge(s_const, 3)
            act.wait_ge(s_small, 48)
            act.activation(tg[:, :], gx[:, :], ACT.Tanh).then_inc(s_tg, 1)

            def weights_high(g, it, u):
                n = piece(g, it, u)
                act.wait_ge(s_wst[u // 2], it * 16 + (g * H // RING * 16 + 16))
                act.copy(wH[:, bass.ds(n * WP, WP)], wst[:, u // 2, :]).then_inc(s_wH, 1)

            def q_pair(g, m):
                act.wait_ge(s_tp, g * GP + m + 1)
                for q in range(2):
                    b = 2 * m + q
                    src = tp[m % 2][:, q * L:(q + 1) * L].rearrange("p (c s i) -> p s c i", c=C, i=HALF)
                    dst = qT[:, :, :, :, b * HALF:(b + 1) * HALF].rearrange("p h s c i -> p (h s) c i")
                    mm = act.copy(dst, src)
                mm.then_inc(s_qT, 1)

            def token_stage(it, u):
                start = isinstance(it, int)
                if u == 0:
                    act.wait_ge(s_tp, it + (NG * GP + 1))
                    if not start:
                        act.wait_ge(s_up, it)
                    act.copy(tH[:, 0, :], tp[0][:, :]).then_inc(s_tH, 1)
                    act.copy(xn[:, bass.ds(it * 2, 2), :], xq[:, 0:2, :]).then_inc(s_kept, 1)
                elif u == 1:
                    act.wait_ge(s_up, it + 1)
                    act.copy(logit[:, bass.ds(it * 2, 2), :].rearrange("p t e -> p (t e)"),
                             att[0][:, ROUTE:ROUTE + 2 * NR]).then_inc(s_logit, 1)
                    silu_pair(tp[1], 0, None if start else it)
                elif u == 2:
                    high_hidden(att[0], 0, it, None if start else it)

            def scores(g):
                act.wait_ge(s_logit, (g + 1) * GP)
                if g:
                    act.wait_ge(s_gates, g)
                act.activation(score[:, :, :], logit[:, :, :], ACT.Sigmoid).then_inc(s_score, 1)

            def root(i, mv):
                act.activation(std[:, i, :], mv[:, :, 1], ACT.Sqrt, bias=epsc[:, :]).then_inc(s_std, 1)

            def tokens_logits():
                for j in range(GP + 1):
                    n = GP + j
                    if j < GP:
                        act.wait_ge(s_tp, A_SLOT - GP + j + 1)
                        if j == 0:
                            act.wait_ge(s_up, GP)
                        if j >= 2:
                            act.wait_ge(s_lg, j - 1)
                        act.copy(tH[:, j % 2, :], tp[j % 2][:, :]).then_inc(s_tH, 1)
                    if j >= 1:
                        act.wait_ge(s_lg, j)
                        if j == 1:
                            act.wait_ge(s_score, 1)
                        act.copy(logit[:, 2 * (j - 1):2 * j, :].rearrange("p t e -> p (t e)"),
                                 hT[(j - 1) % 2][:, ROUTE:ROUTE + 2 * NR]).then_inc(s_logit, 1)

            def silu_pair(bank, p, used):
                if used is not None:
                    act.wait_ge(s_hid, used)
                act.activation(silu[:, p, :, :], bank[:, :].rearrange("p (q b n) -> p q b n", q=2, b=2)[:, :, 0, :],
                               ACT.Silu).then_inc(s_silu, 1)

            def high_hidden(bank, p, n, used):
                act.wait_ge(s_hT, n + 1)
                if used is not None:
                    act.wait_ge(s_down, used)
                act.copy(hTH[:, p, :], bank[:, 0:2 * P]).then_inc(s_hTH, 1)

            def clear_slots():
                for to in xg_d:
                    act.dma_start(to.rearrange("(p r n) d -> p r (n d)", p=P, n=4),
                                  sx[:, :, :].rearrange("p r d -> p (r d)").unsqueeze(1)
                                  .to_broadcast([P, NT // 4, 4 * L])).then_inc(s_xg_zero, 16)

            act.wait_ge(s_mv[0], GB)
            root(0, mv1)
            for m in range(GP):
                q_pair(0, m)
            with act.Fori(0, H // RING) as it:
                for u in (0, 2):
                    weights_high(0, it, u)
            clear_slots()
            act.wait_ge(s_mv[0], NG * GB)
            act.wait_ge(s_z, H + 2)
            root(0, mv1)
            for m in range(GP):
                q_pair(1, m)
            act.wait_ge(s_mv[1], GB)
            root(1, mv2)
            for first, end in ((0, 1), (1, H // RING)):
                with (nullcontext(0) if first == 0 else act.Fori(first, end)) as it:
                    for u in range(RING):
                        if u % 2 == 0:
                            weights_high(1, it, u)
                        token_stage(it, u)
            scores(0)
            act.wait_ge(s_mv[1], NG * GB)
            root(1, mv2)
            tokens_logits()
            scores(1)

            def step(i, u, first=False, last=0):
                j, p = i * RING + u, u % 2

                def used(n):
                    return max(n, N_SLOT) if first else n

                if last == 0:
                    act.wait_ge(s_tp, j + (A_SLOT + 1))
                    if first and j < 2:
                        act.wait_ge(s_lg, GP - 1 + j)
                    else:
                        act.wait_ge(s_up, j + (N_SLOT - 1))
                    act.copy(tH[:, p, :], tp[p][:, :]).then_inc(s_tH, 1)
                if last <= 1 and not (first and j < 1):
                    act.wait_ge(s_up, j + N_SLOT)
                    silu_pair(up[1 - p], 1 - p, used(j + (N_SLOT - 2)))
                if last <= 2 and not (first and j < 2):
                    high_hidden(hT[p], p, j + (N_SLOT - 2), used(j + (N_SLOT - 3)))
                if not (first and j < 3) and not (isinstance(j, int) and j >= NS + 3):
                    act.wait_ge(s_down, j + (N_SLOT - 2))
                    r = (u + 1) % RING
                    if not (first and j < 7):
                        act.wait_ge(s_stored[r], i * 16 + (0 if u == RING - 1 else -16))
                    act.copy(yrow[:, r, :, :].rearrange("p t n -> p (t n)"), yy[1 - p][:, :]).then_inc(s_yrow, 1)

            for i in range(2):
                for u in range(RING):
                    step(i, u, first=True)
            with act.Fori(2, 2 * half) as i:
                for u in range(RING):
                    step(i, u)
            for j in range(NS, NJ + 3):
                step(j // RING, j % RING, last=max(0, j - NJ + 1))

        @block.vector
        def _(dve):
            chain = [0]

            def linked(ins):
                chain[0] += 1
                ins.then_inc(s_rank, 1)
                dve.wait_ge(s_rank, chain[0])

            def mean_var(i, g, mv):
                for b in range(GB):
                    dve.wait_ge(s_st[i], g * GB + b + 1)
                    dve.bn_aggr(mv[:, b, :], stats[:, i, b, :]).then_inc(s_mv[i], 1)

            def top_two(g):
                sc = score[:, :, :].rearrange("p t e -> p (t e)")
                shape = [P, GB, NR, NR]
                mine, other = (score[:, :, :].unsqueeze(d).to_broadcast(shape) for d in (3, 2))
                gt, eq = (v[:, :, :].rearrange("p (t e) f -> p t e f", e=NR) for v in (cgt, ceq))
                dve.wait_ge(s_score, g + 1)
                dve.tensor_tensor(gt, other, mine, ALU.is_gt)
                linked(dve.tensor_tensor(eq, other, mine, ALU.is_equal))
                flat = ceq[:, :, :].rearrange("p (t e) f -> p t (e f)", e=NR)
                linked(dve.tensor_tensor(flat, flat, before.unsqueeze(1).to_broadcast([P, GB, NR * NR]), ALU.mult))
                linked(dve.tensor_tensor(cgt[:, :, :], cgt[:, :, :], ceq[:, :, :], ALU.add))
                linked(dve.tensor_reduce(rank[:, :], cgt[:, :, :], AX.X, ALU.add))
                if g:
                    dve.wait_ge(s_cnt, g)
                dve.tensor_scalar(both[:, :], rank[:, :], float(TOPK), None, ALU.is_lt).then_inc(s_both, 1)
                for k in range(TOPK):
                    ins = dve.tensor_scalar(sel[:, k, :], rank[:, :], float(k), None, ALU.is_equal)
                linked(ins)
                linked(dve.tensor_tensor(pick[:, :, :], sel[:, :, :], sc.unsqueeze(1).to_broadcast([P, TOPK, GB * NR]),
                                         ALU.mult))
                dve.tensor_reduce(gates[:, g, :, :].rearrange("p k t -> p (k t)"),
                                  pick[:, :, :].rearrange("p k (t e) -> p (k t) e", e=NR),
                                  AX.X, ALU.add).then_inc(s_gates, 1)

            def slots(g, p):
                dve.wait_ge(s_cnt, g + 1)
                dve.tensor_copy(cnt[:, :], hT[p][:, ROUTE:ROUTE + (GB + 1) * NR]).then_inc(s_cnt_read, 1)
                dve.wait_ge(s_cnt_read, g + 1)
                total = cnt[:, GB * NR:]
                sq = [P, NR, NR]
                wide = cgt[:, 0:NR, :]
                linked(dve.tensor_tensor(wide, total.unsqueeze(2).to_broadcast(sq), thr.unsqueeze(1).to_broadcast(sq),
                                         ALU.is_gt))
                linked(dve.tensor_reduce(ntile[:, :], wide, AX.X, ALU.add))
                linked(dve.tensor_tensor(wide, before.rearrange("p (e f) -> p e f", f=NR),
                                         ntile[:, :].unsqueeze(1).to_broadcast(sq), ALU.mult))
                linked(dve.tensor_reduce(base[:, :], wide, AX.X, ALU.add))
                linked(dve.scalar_tensor_tensor(
                    out=slot[:, :].rearrange("p (t e) -> p t e", e=NR),
                    in0=base[:, :].unsqueeze(1).to_broadcast([P, GB, NR]), scalar=float(P),
                    in1=cnt[:, 0:GB * NR].rearrange("p (t e) -> p t e", e=NR), op0=ALU.mult, op1=ALU.add))
                linked(dve.tensor_tensor(pick[:, :, :], sel[:, :, :],
                                         slot[:, :].unsqueeze(1).to_broadcast([P, TOPK, GB * NR]), ALU.mult))
                linked(dve.tensor_reduce(slotf[:, :], pick[:, :, :].rearrange("p k (t e) -> p (k t) e", e=NR),
                                         AX.X, ALU.add))
                dve.tensor_copy(idx[:, g, :, :].rearrange("p k t -> p (k t)"), slotf[:, :]).then_inc(s_idx, 1)
                linked(dve.tensor_tensor(ends[:, :], base[:, :], ntile[:, :], ALU.add))
                tall = cgt[:, 0:NT, :]
                shape = [P, NT, NR]
                linked(dve.tensor_tensor(tall, tile_no.unsqueeze(2).to_broadcast(shape),
                                         ends[:, :].unsqueeze(1).to_broadcast(shape), ALU.is_ge))
                linked(dve.tensor_reduce(etf[:, :], tall, AX.X, ALU.add))
                dve.tensor_scalar(etile[:, g, :], etf[:, :], float(NR - 1), float(WE), ALU.min, ALU.mult).then_inc(s_etile, 1)

            def low_tokens(bank, p, n):
                dve.wait_ge(s_tH, n + 1)
                dve.tensor_tensor(tL[:, p, :], bank[:, :], tH[:, p, :].bitcast(F32), ALU.subtract).then_inc(s_tL, 1)

            def hidden(bank, p, n):
                dve.wait_ge(s_silu, n + 1)
                dve.tensor_tensor(hid[:, p, :, :], bank[:, :].rearrange("p (q b n) -> p q b n", q=2, b=2)[:, :, 1, :],
                                  silu[:, p, :, :], ALU.mult).then_inc(s_hid, 1)

            def low_hidden(bank, p, n):
                dve.wait_ge(s_hTH, n + 1)
                dve.tensor_tensor(hTL[:, p, :], bank[:, 0:2 * P], hTH[:, p, :].bitcast(F32),
                                  ALU.subtract).then_inc(s_hTL, 1)

            def shared(bank, t):
                xp = xs[:, bass.ds(t, 2), :].rearrange("p t n -> p (t n)")
                dve.scalar_tensor_tensor(out=xp, in0=bank[:, :], scalar=tg[:, 1:2], in1=xp,
                                         op0=ALU.mult, op1=ALU.add).then_inc(s_shared, 1)

            def norm_q(g, b):
                if b >= 4:
                    dve.wait_ge(s_tp, g * GP + b // 2 - 1)
                dve.tensor_scalar(xq[:, b % 4, :], xs[:, g * GB + b, :], mv1[:, b, 0:1], rstd[:, 0, b:b + 1],
                                  ALU.subtract, ALU.mult).then_inc(s_xq, 1)

            def norm_pair(g, m, to):
                for q in range(2):
                    b = m * 2 + q
                    dve.tensor_scalar(to[:, q, :], xs[:, bass.ds(b + g * GB, 1), :].rearrange("p t n -> p (t n)"),
                                      mv2[:, bass.ds(b, 1), 0:1].rearrange("p t n -> p (t n)"),
                                      rstd[:, 1, bass.ds(b, 1)], ALU.subtract, ALU.mult).then_inc(s_xn, 1)

            def attended(g, m):
                j = g * GP + m
                xp = xs[:, 2 * j:2 * j + 2, :].rearrange("p t n -> p (t n)")
                dve.wait_ge(s_isum, j + 1)
                dve.scalar_tensor_tensor(out=xp, in0=att[m % 2][:, :], scalar=tg[:, 0:1], in1=xp,
                                         op0=ALU.mult, op1=ALU.add).then_inc(s_x2, 1)

            def statistics(g, m):
                dve.wait_ge(s_x2, g * GP + m + 1)
                for b in (2 * m, 2 * m + 1):
                    dve.bn_stats(stats[:, 1, b, :], xs[:, g * GB + b, :]).then_inc(s_st[1], 1)

            def head(g, it, u):
                h = it * RING + u
                yd = yD[u % 2][:, 0:DCOLS].rearrange("p (s n j) -> p s n j", s=2, j=HALF)
                yo = yO[u % 2][:, 0:OCOLS].rearrange("p (n j) -> p n j", j=HALF)
                q_h = qT[:, bass.ds(h, 1), :, :, :].rearrange("p h s c n -> p s (h c n)")
                zh = z[:, :, :, bass.ds(h * HD, HD)]
                ni = CB * HALF
                dve.wait_ge(s_conv, h + (g * H + 1 + RING))
                dve.tensor_tensor(zh[:, 0, :, :].rearrange("p n (s j) -> p s n j", s=2), yd,
                                  q_h.unsqueeze(3).to_broadcast([P, 2, ni, HALF]), ALU.mult)
                dve.tensor_tensor(zh[:, 1, :, HALF:], yo,
                                  q_h[:, 0, :].unsqueeze(2).to_broadcast([P, ni, HALF]), ALU.mult)
                q_j = q_h[:, 1, :].rearrange("p (n j) -> p n j", j=HALF)
                dve.tensor_tensor(zh[:, 1, :, 0:HALF].rearrange("p (n j) i -> p n i j", j=HALF),
                                  yo.rearrange("p (n i) j -> p n i j", i=HALF),
                                  q_j.unsqueeze(2).to_broadcast([P, CB, HALF, HALF]),
                                  ALU.mult).then_inc(s_z, 1)
                if u % 2 == 0:
                    n = piece(g, it, u)
                    dve.wait_ge(s_wH, n + 1)
                    dve.tensor_tensor(wL[:, bass.ds(n * WP, WP)], wst[:, u // 2, :],
                                      wH[:, bass.ds(n * WP, WP)].bitcast(F32), ALU.subtract).then_inc(s_wL, 1)

            def token_stage(it, u):
                start = isinstance(it, int)
                if u == 0:
                    if not start:
                        dve.wait_ge(s_up, it)
                    low_tokens(tp[0], 0, it)
                elif u == 1:
                    if not start:
                        dve.wait_ge(s_hT, it)
                    hidden(tp[1], 0, it)
                elif u == 2:
                    if not start:
                        dve.wait_ge(s_down, it)
                    low_hidden(att[0], 0, it)
                else:
                    dve.wait_ge(s_down, it + 1)
                    shared(att[1], it * 2)

            def tokens_logits():
                for j in range(-1, GP):
                    if j + 1 < GP:
                        t = GB + 2 * (j + 1)
                        norm_pair(1, j + 1, xn[:, t:t + 2, :])
                    if j >= 0:
                        if j == 0:
                            dve.wait_ge(s_up, GP)
                        if j >= 2:
                            dve.wait_ge(s_lg, j - 1)
                        low_tokens(tp[j % 2], j % 2, GP + j)

            dve.sem_inc(s_z, 2)
            dve.sem_inc(s_wL, 2)
            dve.wait_ge(s_kp, 32)
            dve.tensor_tensor(kp[:, P - 1:P], kp[:, P - 1:P], dsk[:, :], ALU.add).then_inc(s_kpd, 1)
            dve.wait_ge(s_x[0], 16)
            for b in range(GB):
                dve.bn_stats(stats[:, 0, b, :], xs[:, b, :]).then_inc(s_st[0], 1)
            mean_var(0, 0, mv1)
            dve.wait_ge(s_std, 1)
            linked(dve.reciprocal(rstd[:, 0, :], std[:, 0, :]))
            for b in range(GB):
                norm_q(0, b)
            dve.wait_ge(s_small, 48)
            dve.tensor_copy(upper[:, :], const[:, K_UP:K_UP + P]).then_inc(s_upper, 1)
            linked(dve.tensor_copy(gwH[:, :], gw[:, :]))
            dve.tensor_tensor(gwL[:, :], gw[:, :], gwH[:, :].bitcast(F32), ALU.subtract).then_inc(s_gw, 2)
            dve.wait_ge(s_qT, GP)
            dve.wait_ge(s_mv[0], GB)
            dve.wait_ge(s_x[1], 16)
            with dve.Fori(0, H // RING) as it:
                for u in range(RING):
                    head(0, it, u)
                    if u % 2:
                        b = it * 2 + u // 2
                        dve.bn_stats(stats[:, 0, b, :], xs[:, b + GB, :]).then_inc(s_st[0], 1)
            dve.wait_ge(s_xq, GB)
            mean_var(0, 1, mv1)
            dve.wait_ge(s_std, 2)
            linked(dve.reciprocal(rstd[:, 0, :], std[:, 0, :]))
            dve.wait_ge(s_tg, 1)
            for m in range(GP):
                norm_q(1, 2 * m)
                norm_q(1, 2 * m + 1)
                attended(0, m)
                if m:
                    statistics(0, m - 1)
            statistics(0, GP - 1)
            mean_var(1, 0, mv2)
            dve.wait_ge(s_std, 3)
            linked(dve.reciprocal(rstd[:, 1, :], std[:, 1, :]))
            dve.wait_ge(s_tp, NG * GP)
            norm_pair(0, 0, xq)
            dve.wait_ge(s_isum, GP)
            dve.wait_ge(s_qT, NG * GP)
            for first, end in ((0, 1), (1, H // RING)):
                with (nullcontext(0) if first == 0 else dve.Fori(first, end)) as it:
                    if first:
                        dve.wait_ge(s_tp, it + NG * GP)
                        dve.wait_ge(s_kept, it)
                        norm_pair(0, it, xq)
                    for u in range(RING):
                        head(1, it, u)
                        token_stage(it, u)
            dve.wait_ge(s_tp, A_SLOT - GP)
            dve.wait_ge(s_kept, GP)
            top_two(0)
            for m in range(GP):
                attended(1, m)
                if m == 0:
                    dve.wait_ge(s_xn, GB)
                else:
                    statistics(1, m - 1)
                if m == 1:
                    slots(0, 0)
            statistics(1, GP - 1)
            mean_var(1, 1, mv2)
            dve.wait_ge(s_std, 4)
            linked(dve.reciprocal(rstd[:, 1, :], std[:, 1, :]))
            tokens_logits()
            top_two(1)

            def step(i, u, first=False, last=0):
                j, p = i * RING + u, u % 2

                def used(n):
                    return max(n, N_SLOT) if first else n

                if last == 0:
                    if first and j < 2:
                        dve.wait_ge(s_lg, GP - 1 + j)
                    else:
                        dve.wait_ge(s_up, j + (N_SLOT - 1))
                    low_tokens(tp[p], p, j + T_SLOT)
                if last <= 1 and not (first and j < 1):
                    dve.wait_ge(s_hT, used(j + (N_SLOT - 2)))
                    hidden(up[1 - p], 1 - p, j + (N_SLOT - 1))
                if last <= 2 and not (first and j < 2):
                    dve.wait_ge(s_down, used(j + (N_SLOT - 3)))
                    low_hidden(hT[p], p, j + (N_SLOT - 2))
                if isinstance(j, int) and j >= NS + 3:
                    dve.wait_ge(s_down, j + (N_SLOT - 2))
                    shared(yy[1 - p], GB + 2 * (j - 3 - NS))

            for u in range(RING):
                step(0, u, first=True)
                if u == 1:
                    slots(1, 0)
            with dve.Fori(1, 2 * half) as i:
                for u in range(RING):
                    step(i, u)
            for j in range(NS, NJ + 3):
                step(j // RING, j % RING, last=max(0, j - NJ + 1))

            dve.wait_ge(s_shared, NG * GP)
            for t in range(B):
                dve.wait_ge(s_got[t], 16 * TOPK)
                dve.tensor_tensor(got[:, t, 0, :], got[:, t, 0, :], got[:, t, 1, :], ALU.add).then_inc(s_sum, 1)
                dve.wait_ge(s_sum, t + 1)
                dve.scalar_tensor_tensor(out=xs[:, t, :], in0=got[:, t, 0, :], scalar=tg[:, 1:2], in1=xs[:, t, :],
                                         op0=ALU.mult, op1=ALU.add).then_inc(s_fin, 1)


def constants(np):
    k = np.zeros((P, NK), np.float32)
    k[:, K_ID:K_ID + P] = np.eye(P)
    k[:, K_UP:K_UP + P] = np.triu(np.ones((P, P)), 1)
    k[:, K_BEF:K_BEF + NR * NR] = np.tril(np.ones((NR, NR)), -1).reshape(-1)
    k[:, K_THR:K_THR + NR] = P * np.arange(NR)
    k[:, K_TILE:K_TILE + NT] = np.arange(NT)
    return k


def kernel(x, ctx_2048, g_xattn, g_ffn, L0_xattn_ssm_kernel, L0_xattn_D, L0_ffn_gate_w,
           L0_ffn_w1, L0_ffn_w2, L0_ffn_w3, L0_ffn_ws1, L0_ffn_ws2, L0_ffn_ws3):
    import numpy as np
    import concourse.bacc as bacc
    from concourse.bass_utils import run_bass_kernel_spmd as run

    cont = np.ascontiguousarray
    a = [np.asarray(v) for v in (x, ctx_2048, g_xattn, g_ffn, L0_xattn_ssm_kernel, L0_xattn_D, L0_ffn_gate_w,
                                 L0_ffn_w1, L0_ffn_w2, L0_ffn_w3, L0_ffn_ws1, L0_ffn_ws2, L0_ffn_ws3)]
    x, cx, gxa, gff, ssm, dsk, gate, w1, w2, w3, ws1, ws2, ws3 = a
    kt = cx.reshape(NG, GB, H, 2, HALF, C, P)[..., ::-1].transpose(6, 0, 2, 3, 5, 1, 4)
    kpad = np.zeros((H, KPAD), ssm.dtype)
    kpad[:, P - 1:] = ssm
    up = np.stack([np.concatenate([ws1[None], w1]), np.concatenate([ws3[None], w3])], 1)
    up = up.reshape(NE, 2, HID, C, P).transpose(4, 0, 3, 1, 2).reshape(P, NE, C * 2 * HID)
    down = np.concatenate([ws2[None], w2]).transpose(2, 0, 1)
    w_all = np.concatenate([up, down], 2)
    arrays = {
        "x": cont(x.transpose(1, 0, 2)),
        "kt": cont(kt).reshape(P, NG, H * 2 * CB * HALF),
        "kpad": kpad,
        "d_skip": cont(dsk.reshape(H, 1)),
        "g_both": cont(np.concatenate([gxa, gff]).reshape(1, 2)),
        "gate_w": cont(gate.reshape(NR, C, P).transpose(2, 1, 0)).reshape(P, C * NR),
        "w_all": cont(w_all).reshape(P, NPIECE, WP),
        "consts": constants(np),
    }
    nc = bacc.Bacc("TRN2", target_bir_lowering=False, num_devices=1)
    ins = [nc.dram_tensor(f"in_{n}", v.shape, F32, kind="ExternalInput").ap() for n, v in arrays.items()]
    xg_d = [nc.dram_tensor(f"xg_d{g}", (NT * P, L), F32, kind="Internal").ap() for g in range(NG)]
    y_d = [nc.dram_tensor(f"y_d{g}", (NT * P, L), F32, kind="Internal").ap() for g in range(NG)]
    kpad_d = nc.dram_tensor("kpad_d", (H, KPAD), F32, kind="Internal").ap()
    out = nc.dram_tensor("out", (P, B, L), F32, kind="ExternalOutput").ap()
    build(nc, *ins, kpad_d, xg_d, y_d, out)
    r = run(nc, [{f"in_{n}": v for n, v in arrays.items()}], core_ids=[0])
    return cont(r.results[0]["out"].transpose(1, 0, 2))
```

```python
from contextlib import ExitStack, nullcontext

import concourse.bass as bass
from concourse import mybir

F32 = mybir.dt.float32
F32R = mybir.dt.float32r
BF16 = mybir.dt.bfloat16
I32 = mybir.dt.int32
U32 = mybir.dt.uint32
ALU = mybir.AluOpType
ACT = mybir.ActivationFunctionType
AX = mybir.AxisListType

P = 128
B, L, H, HD = 16, 256, 16, 8
C = L // P
HALF = HD // 2
NG, GB = 2, B // 2
CB = C * GB
NR = 8
NE, HID = NR + 1, 128
TOPK = 2
EPS = 1e-5
KPAD = P - 1 + L
RING = 4
WE = C * 2 * HID + L
NPIECE = H
WP = NE * WE // NPIECE
DCOLS = 2 * CB * HALF * HALF
OCOLS = CB * HALF * HALF
GP = GB // 2
NT = 24
SP = NT // 2
NS = NG * SP
SHARED = 0
K_ID, K_UP, K_BEF, K_THR, K_TILE = 0, P, 2 * P, 2 * P + NR * NR, 2 * P + NR * NR + NR
NK = K_TILE + NT


def build(nc, x, kt, kpad, d_skip, g_both, gate_w, w_all, consts, kpad_d, xg_d, y_d, out):
    with ExitStack() as ctx:
        def sb(name, shape, dt=F32, stack=ctx):
            return stack.enter_context(nc.sbuf_tensor(name, shape, dt))

        def psum(name):
            return ctx.enter_context(nc.psum_tensor(name, [P, 512], F32))

        def sem(name):
            return ctx.enter_context(nc.semaphore(name))

        xs = sb("xs", [P, B, L])
        toep = sb("toep", [P, RING, L])
        kv = sb("kv", [P, 2, DCOLS + OCOLS])
        wH = sb("wH", [P, NE * WE], F32R)
        wL = sb("wL", [P, NE * WE], F32R)
        gw = sb("gw", [P, C * NR])
        gwHL = sb("gwHL", [P, C, 2, NR], F32R)
        xq = sb("xq", [P, 4, L])
        xn = sb("xn", [P, B, L])
        early = xn[:, GB:, :].rearrange("p t n -> p (t n)")
        wst = early[:, 0:2 * WP].rearrange("p (u n) -> p u n", u=2)
        kp = early[0:H, 2 * WP:2 * WP + KPAD]
        dsk = early[0:H, 2 * WP + KPAD:2 * WP + KPAD + 1]
        stats = sb("stats", [P, 2, GB, 6])
        mv1 = sb("mv1", [P, GB, 2])
        mv2 = sb("mv2", [P, GB, 2])
        std = sb("std", [P, 2, GB])
        rstd = sb("rstd", [P, 2, GB])
        gx = sb("gx", [P, 2])
        tg = sb("tg", [P, 2])
        const = sb("const", [P, NK])
        ident = const[:, K_ID:K_ID + P]
        before = const[:, K_BEF:K_BEF + NR * NR]
        thr = const[:, K_THR:K_THR + NR]
        tile_no = const[:, K_TILE:K_TILE + NT]
        upper = sb("upper", [P, P], BF16)
        ones = sb("ones", [P, P], BF16)
        epsc = sb("epsc", [P, 1])
        unused = sb("unused", [P, 1])
        tH = sb("tH", [P, 2, 2 * L], F32R)
        tL = sb("tL", [P, 2, 2 * L], F32R)
        silu = sb("silu", [P, 2, 2, HID])
        hid = sb("hid", [P, 2, 2, HID])
        hTH = sb("hTH", [P, 2, 2 * P], F32R)
        hTL = sb("hTL", [P, 2, 2 * P], F32R)
        lt = sb("lt", [2 * NR, GB * P])
        logit = sb("logit", [P, GB, NR])
        score = sb("score", [P, GB, NR])
        cgt, ceq = (xq[:, v, :].bitcast(BF16).rearrange("p (b f) -> p b f", f=NR) for v in range(2))
        earlier = sb("earlier", [P, NR * NR], BF16)
        rank = sb("rank", [P, GB * NR])
        sel = sb("sel", [P, TOPK, GB * NR])
        both = sb("both", [P, GB * NR], BF16)
        pick = sb("pick", [P, TOPK, GB * NR])
        gates = sb("gates", [P, NG, TOPK, GB])
        cnt = sb("cnt", [P, (GB + 1) * NR])
        ntile = sb("ntile", [P, NR])
        base = sb("base", [P, NR])
        ends = sb("ends", [P, NR])
        slot = sb("slot", [P, GB * NR])
        slotf = sb("slotf", [P, TOPK * GB])
        etf = sb("etf", [P, NT])
        etile = sb("etile", [P, NG, NT], I32)
        idx = sb("idx", [P, NG, TOPK, GB], U32)
        zero = sb("zero", [P, L])
        with ExitStack() as stage1:
            kT = sb("kT", [P, H, 2 * CB * HALF], F32, stage1)
            qT = sb("qT", [P, H, 2, C, GB * HALF], F32, stage1)
            z = sb("z", [P, 2, CB * HALF, P], F32, stage1)
        sx = sb("sx", [P, GB * TOPK, L])
        got = sb("got", [P, B, TOPK, L])
        xrow = sb("xrow", [P, RING, 2, L])
        yrow = sb("yrow", [P, RING, 2, L])

        yD = [psum(f"yD{i}") for i in range(2)]
        yO = [psum(f"yO{i}") for i in range(2)]
        att = [psum(f"att{i}") for i in range(2)]
        tp = [psum(f"tp{i}") for i in range(2)]
        up, hT, yy = yD, yO, att
        ROUTE = 2 * P

        s_kt = [sem(f"s_kt{i}") for i in range(3)]
        s_x = [sem(f"s_x{i}") for i in range(3)]
        s_kp = sem("s_kp")
        s_small = sem("s_small")
        s_kpd = sem("s_kpd")
        s_kpd_stored = sem("s_kpd_stored")
        s_toep = [sem(f"s_toep{u}") for u in range(RING)]
        s_wst = [sem(f"s_wst{u}") for u in range(2)]
        s_zero = sem("s_zero")
        s_const = sem("s_const")
        s_upper = sem("s_upper")
        s_kv = sem("s_kv")
        s_conv = sem("s_conv")
        s_z = sem("s_z")
        s_isum = sem("s_isum")
        s_attended = sem("s_attended")
        s_tg = sem("s_tg")
        s_st = [sem(f"s_st{i}") for i in range(2)]
        s_mv = [sem(f"s_mv{i}") for i in range(2)]
        s_std = sem("s_std")
        s_rstd = sem("s_rstd")
        s_xq = sem("s_xq")
        s_xn = sem("s_xn")
        s_tp = sem("s_tp")
        s_qT = sem("s_qT")
        s_wH = sem("s_wH")
        s_wL = sem("s_wL")
        s_gw = sem("s_gw")
        s_tH = sem("s_tH")
        s_tL = sem("s_tL")
        s_up = sem("s_up")
        s_logit = sem("s_logit")
        s_lt = sem("s_lt")
        s_rows = sem("s_rows")
        s_lg = sem("s_lg")
        s_score = sem("s_score")
        s_rank = sem("s_rank")
        s_both = sem("s_both")
        s_gates = sem("s_gates")
        s_cnt = sem("s_cnt")
        s_cnt_read = sem("s_cnt_read")
        s_slot = sem("s_slot")
        s_etile = sem("s_etile")
        s_idx = sem("s_idx")
        s_xg_zero = [sem(f"s_xg_zero{g}") for g in range(NG)]
        s_sx = sem("s_sx")
        s_sent = [sem(f"s_sent{g}") for g in range(NG)]
        s_xrow = [sem(f"s_xrow{r}") for r in range(RING)]
        s_silu = sem("s_silu")
        s_hid = sem("s_hid")
        s_hT = sem("s_hT")
        s_hTH = sem("s_hTH")
        s_hTL = sem("s_hTL")
        s_down = sem("s_down")
        s_shared = sem("s_shared")
        s_yrow = sem("s_yrow")
        s_stored = [sem(f"s_stored{r}") for r in range(RING)]
        s_got = [sem(f"s_got{t}") for t in range(B)]
        s_sum = sem("s_sum")
        s_fin = sem("s_fin")
        s_out = sem("s_out")

        block = ctx.enter_context(nc.Block())

        A_SLOT, T_SLOT = 2 * NG * GP, NG * GP
        TOK = 2 * GP
        half = SP // RING
        NJ = NS + NG * GP

        def order(j):
            return {NS: "BCDA", NS + 1: "CDAB", NS + 2: "DABC"}.get(j, "ABCD") if isinstance(j, int) else "ABCD"

        def piece(g, it, u):
            return it * 2 + (g * H // 2 + u // 2)

        @block.sync
        def _(sp):
            sp.dma_start(kp[:, :], kpad).then_inc(s_kp, 16)
            sp.dma_start(dsk[:, :], d_skip).then_inc(s_kp, 16)
            sp.dma_start(const[:, :], consts).then_inc(s_small, 16)
            sp.wait_ge(s_kpd, 1)
            sp.dma_start(kpad_d, kp[:, :]).then_inc(s_kpd_stored, 16)
            for i in range(2):
                heads = slice(i * H // 2, (i + 1) * H // 2)
                sp.dma_start(kT[:, heads, :], kt[:, 0, :].rearrange("p (h n) -> p h n", h=H)[:, heads, :]
                             ).then_inc(s_kt[i], 16)
            sp.wait_ge(s_kpd_stored, 16)
            toep_rows = bass.AP(tensor=kpad_d.tensor, offset=0, ap=[[KPAD, H], [1, P], [1, L]])
            for g in range(NG):
                with sp.Fori(0, H // RING) as it:
                    for u in range(RING):
                        h = it * RING + u
                        sp.wait_ge(s_conv, h + (g * H + 1))
                        sp.dma_start(toep[:, u, :], toep_rows[h]).then_inc(s_toep[u], 16)
                        if u % 2 == 0:
                            n = piece(g, it, u)
                            sp.wait_ge(s_wL, n + 1)
                            sp.dma_start(wst[:, u // 2, :], w_all[:, n, :]).then_inc(s_wst[u // 2], 16)
                if g == 0:
                    sp.wait_ge(s_kv, H)
                    sp.dma_start(kT[:, :, :].rearrange("p h n -> p (h n)"), kt[:, 1, :]).then_inc(s_kt[2], 16)

            def load(i, u, g):
                rows = xg_d[g].rearrange("(j t p) d -> j p t d", t=2, p=P)
                sp.wait_ge(s_tp, i * RING + (A_SLOT + u + 1 - RING))
                sp.dma_start(xrow[:, u, :, :], rows[i * RING + (u - g * SP)]).then_inc(s_xrow[u], 16)

            def store(i, u, g):
                rows = y_d[g].rearrange("(j t p) d -> j p t d", t=2, p=P)
                sp.wait_ge(s_yrow, i * RING + (u + 1 - 2 * RING))
                sp.dma_start(rows[i * RING + (u - 2 * RING - g * SP)], yrow[:, u, :, :]).then_inc(s_stored[u], 16)

            for first, end, g_load, g_store in ((0, 2, 0, None), (2, half, 0, 0), (half, half + 2, 1, 0),
                                                (half + 2, 2 * half, 1, 1), (2 * half, 2 * half + 2, None, 1)):
                if first in (0, half):
                    sp.wait_ge(s_sent[g_load], 16 * GB * TOPK)
                with sp.Fori(first, end) as i:
                    for u in range(RING):
                        if g_load is not None:
                            load(i, u, g_load)
                        if g_store is not None:
                            store(i, u, g_store)
            with sp.Fori(0, B // 2) as i:
                sp.wait_ge(s_shared, i + 1)
                for q in range(2):
                    t = i * 2 + q
                    sp.wait_ge(s_fin, t + 1)
                    sp.dma_start(out[:, t, :], xs[:, t, :]).then_inc(s_out, 16)
            sp.wait_ge(s_out, 16 * B)

        @block.gpsimd
        def _(pool):
            pool.memset(ones[:, :], 1.0).then_inc(s_const, 1)
            pool.memset(epsc[:, :], EPS).then_inc(s_const, 1)
            pool.memset(zero[:, :], 0.0).then_inc(s_const, 1)
            for g, first, end, loaded in (0, 0, H // 4, s_kt[0]), (0, H // 4, H // 2, s_kt[1]), (1, 0, H // 2, s_kt[2]):
                pool.wait_ge(loaded, 16)
                with pool.Fori(first, end) as it:
                    for u in range(2):
                        k_h = kT[:, it * 2 + u, :].rearrange("p (s i) -> p s i", i=HALF)
                        kd = kv[:, u, 0:DCOLS].rearrange("p (s i j) -> p s i j", i=HALF, j=HALF)
                        ko = kv[:, u, DCOLS:].rearrange("p (s i j) -> p s i j", i=HALF, j=HALF)
                        full, off = [P, 2 * CB, HALF, HALF], [P, CB, HALF, HALF]
                        pool.wait_ge(s_conv, it * 2 + (g * H + u + RING - 1))
                        pool.tensor_tensor(kd, k_h.unsqueeze(3).to_broadcast(full),
                                           k_h.unsqueeze(2).to_broadcast(full), ALU.mult)
                        pool.tensor_tensor(ko, k_h[:, 0:CB, :].unsqueeze(3).to_broadcast(off),
                                           k_h[:, CB:2 * CB, :].unsqueeze(2).to_broadcast(off),
                                           ALU.mult).then_inc(s_kv, 1)
            for g in range(NG):
                pool.wait_ge(s_xg_zero[g], 16)
                pool.wait_ge(s_idx, g + 1)
                for t in range(GB):
                    for k in range(TOPK):
                        n = t * TOPK + k
                        pool.wait_ge(s_sx, g * GB * TOPK + n + 1)
                        pool.indirect_dma_start(
                            out=xg_d[g], out_offset=bass.IndirectOffsetOnAxis(ap=idx[:, g, k, t:t + 1], axis=0),
                            in_=sx[:, n, :], in_offset=None).then_inc(s_sent[g], 16)
            for g in range(NG):
                for r in range(RING):
                    pool.wait_ge(s_stored[r], 16 * (g + 1) * SP // RING)
                for t in range(GB):
                    for k in range(TOPK):
                        pool.indirect_dma_start(
                            out=got[:, g * GB + t, k, :], out_offset=None, in_=y_d[g],
                            in_offset=bass.IndirectOffsetOnAxis(ap=idx[:, g, k, t:t + 1], axis=0),
                        ).then_inc(s_got[g * GB + t], 16)

        @block.tensor
        def _(pe):
            def stage_a(bank, src):
                for q in range(2):
                    for c in range(C):
                        mm = pe.transpose(bank[:, q * L + c * P:q * L + (c + 1) * P],
                                          src(q)[:, c * P:(c + 1) * P], ident)
                mm.then_inc(s_tp, 1)

            def three(o, aH, aL, w, start, stop):
                pe.matmul(o, aH, wH[:, w], start=start, stop=False)
                pe.matmul(o, aH, wL[:, w], start=False, stop=False)
                return pe.matmul(o, aL, wH[:, w], start=False, stop=stop)

            def stage_b(bank, p, experts):
                for q, e in enumerate(experts):
                    for c in range(C):
                        cols = slice(q * L + c * P, q * L + (c + 1) * P)
                        mm = three(bank[:, q * L:(q + 1) * L], tH[:, p, cols], tL[:, p, cols],
                                   bass.ds(e + c * 2 * HID, 2 * HID), c == 0, c == C - 1)
                mm.then_inc(s_up, 1)

            def stage_c(bank, p):
                for q in range(2):
                    mm = pe.transpose(bank[:, q * P:(q + 1) * P], hid[:, p, q, :], ident)
                mm.then_inc(s_hT, 1)

            def stage_d(bank, p, experts):
                for q, e in enumerate(experts):
                    cols = slice(q * P, (q + 1) * P)
                    mm = three(bank[:, q * L:(q + 1) * L], hTH[:, p, cols], hTL[:, p, cols],
                               bass.ds(e + C * 2 * HID, L), True, True)
                mm.then_inc(s_down, 1)

            def logits(bank, p):
                for c in range(C):
                    high, low = (v[:, p, :].rearrange("p (q c n) -> p q c n", q=2, c=C)[:, :, c, :] for v in (tH, tL))
                    pe.matmul(bank[0:2 * NR, 0:2 * P], gwHL[:, c, :, :].rearrange("p v e -> p (v e)"), high,
                              start=(c == 0), stop=False)
                    mm = pe.matmul(bank[0:NR, 0:2 * P], gwHL[:, c, 0, :], low, start=False, stop=(c == C - 1))
                mm.then_inc(s_lg, 1)

            def logit_rows(g, bank):
                pe.wait_ge(s_lt, (g + 1) * GP)
                for t in range(GB):
                    o = ROUTE + t * 2 * NR
                    mm = pe.transpose(bank[:, o:o + 2 * NR], lt[:, t * P:(t + 1) * P], ident[0:2 * NR, 0:2 * NR])
                mm.then_inc(s_rows, 1)

            def q_pair(g, m):
                pe.wait_ge(s_xq, g * GB + 2 * m + 2)
                if g * GP + m >= 2:
                    pe.wait_ge(s_qT, g * GP + m - 1)
                stage_a(tp[m % 2], lambda q: xq[:, (2 * m + q) % 4, :])

            def token_stage(n):
                m = n // 2
                if n % 2 == 0:
                    pe.wait_ge(s_xn, 2 * m + 2)
                    pe.wait_ge(*((s_tL, m) if m else (s_qT, NG * GP)))
                    stage_a(tp[0], lambda q: xn[:, 2 * m + q, :])
                else:
                    pe.wait_ge(s_tL, m + 1)
                    if m == 0:
                        pe.wait_ge(s_attended, GP)
                        pe.wait_ge(s_gw, 2)
                    else:
                        pe.wait_ge(s_lt, m)
                    logits(att[0], 0)

            def count(g, bank):
                pe.wait_ge(s_both, g + 1)
                place = bank[:, ROUTE:ROUTE + GB * NR]
                total = bank[:, ROUTE + GB * NR:ROUTE + (GB + 1) * NR]
                pe.matmul(place, upper[:, :], both[:, :], start=True, stop=False)
                for t in range(GB - 1):
                    later = GB - 1 - t
                    row = both[:, t * NR:(t + 1) * NR].unsqueeze(1).to_broadcast([P, later, NR])
                    pe.matmul(place[:, (t + 1) * NR:].rearrange("p (t e) -> p t e", e=NR), ones[:, :], row,
                              start=False, stop=(t == GB - 2))
                for t in range(GB):
                    mm = pe.matmul(total, ones[:, :], both[:, t * NR:(t + 1) * NR], start=(t == 0),
                                   stop=(t == GB - 1))
                mm.then_inc(s_cnt, 1)

            def conv(g, it, u):
                n = it * RING + (g * H + u)
                pe.wait_ge(s_toep[u], it * 16 + 16 * (g * H // RING + 1))
                pe.wait_ge(s_kv, n + 1)
                pe.wait_ge(s_z, n + 1)
                A, BB, kvu = toep[:, u, 0:P], toep[:, u, P:L], kv[:, u % 2, :]
                yd, yo = yD[u % 2][:, 0:DCOLS], yO[u % 2][:, 0:OCOLS]
                kd, ko = kvu[:, 0:DCOLS], kvu[:, DCOLS:]
                pe.matmul(yd, A, kd, start=True, stop=False)
                pe.matmul(yo, A, ko, start=True, stop=False)
                yd, kd = (v.rearrange("p (s c n) -> p s c n", s=2, c=C) for v in (yd, kd))
                yo, ko = (v.rearrange("p (c n) -> p c n", c=C) for v in (yo, ko))
                pe.matmul(yd[:, :, 1, :], BB, kd[:, :, 0, :], start=False, stop=True)
                pe.matmul(yo[:, 1, :], BB, ko[:, 0, :], start=False, stop=True).then_inc(s_conv, 1)

            def isum(g, m):
                for q in range(2):
                    for c in range(C):
                        for i in range(HD):
                            mm = pe.matmul(att[m % 2][:, q * L + c * P:q * L + (c + 1) * P],
                                           z[:, i // HALF, (c * GB + 2 * m + q) * HALF + i % HALF, :],
                                           ident, is_transpose=True, start=(i == 0), stop=(i == HD - 1))
                mm.then_inc(s_isum, 1)

            pe.sem_inc(s_conv, RING)
            pe.wait_ge(s_small, 48)
            for m in range(GP):
                q_pair(0, m)
            with pe.Fori(0, H // RING) as it:
                for u in range(RING):
                    conv(0, it, u)
            pe.wait_ge(s_z, H + 2)
            for m in range(GP):
                if m >= 2:
                    pe.wait_ge(s_attended, m - 1)
                isum(0, m)
                q_pair(1, m)
            for n in range(TOK):
                conv(1, n // RING, n % RING)
                token_stage(n)
            conv(1, TOK // RING, 0)
            logit_rows(0, att[0])
            for u in range(1, RING):
                conv(1, TOK // RING, u)
            with pe.Fori(TOK // RING + 1, H // RING) as it:
                for u in range(RING):
                    conv(1, it, u)
            count(0, tp[0])
            pe.wait_ge(s_z, NG * H + 2)
            def token_rows(j):
                pe.wait_ge(s_xn, 2 * (GP + j) + 2)
                if j == 0:
                    pe.wait_ge(s_cnt_read, 1)
                elif j >= 2:
                    pe.wait_ge(s_tL, GP + j - 1)
                stage_a(tp[j % 2], lambda q: xn[:, GB + 2 * j + q, :])

            def token_logits(j):
                pe.wait_ge(s_tL, GP + j + 1)
                if j >= 2:
                    pe.wait_ge(s_lt, GP + j - 1)
                logits(hT[j % 2], j % 2)

            for m in range(GP):
                if m >= 2:
                    pe.wait_ge(s_attended, GP + m - 1)
                isum(1, m)
                if m >= 2:
                    token_rows(m - 2)
                if m >= 3:
                    token_logits(m - 3)
            for j in range(GP - 2, GP):
                token_rows(j)
                token_logits(j - 1)
            token_logits(GP - 1)
            logit_rows(1, hT[0])

            def experts(i, first, end):
                n = 2 * (end - first)
                tiles = etile_flat[0:1, 2 * (RING * i + first):2 * (RING * i + end)] if isinstance(i, int) \
                    else etile_flat[0:1, bass.ds(i * (2 * RING) + 2 * first, n)]
                _, v = nc.values_load_multi_w_load_instructions(
                    tiles, engines=[mybir.EngineType.PE], min_val=0, max_val=(NR - 1) * WE,
                    skip_runtime_bounds_check_because="slots() clamps the tile's expert to the last one")
                return {first + k: [e + WE for e in v[2 * k:2 * k + 2]] for k in range(n // 2)}

            etile_flat = etile[:, :, :].rearrange("p g t -> p (g t)")

            def step(i, u, e, first=False, last=0):
                j, p = i * RING + u, u % 2
                tokens = isinstance(j, int) and j >= NS
                for stage in order(j):
                    if stage == "A" and last == 0:
                        if not tokens:
                            pe.wait_ge(s_xrow[u], i * 16 + 16)
                        pe.wait_ge(s_tL, j + (T_SLOT - 1))
                        stage_a(tp[p], lambda q: xn[:, 2 * (j - NS) + q, :] if tokens else xrow[:, u, q, :])
                    elif stage == "B" and last <= 1 and not (first and j < 1):
                        pe.wait_ge(s_tL, j + T_SLOT)
                        if not (first and j < 3):
                            pe.wait_ge(s_hid, j - 2)
                        stage_b(up[1 - p], 1 - p, e[j - 1 if tokens else u - 1])
                    elif stage == "C" and last <= 2 and not (first and j < 2):
                        pe.wait_ge(s_hid, j - 1)
                        if not (first and j < 4):
                            pe.wait_ge(s_hTL, j - 3)
                        stage_c(hT[p], p)
                    elif stage == "D" and not (first and j < 3):
                        pe.wait_ge(s_hTL, j - 2)
                        if tokens and j >= NS + 5:
                            pe.wait_ge(s_shared, j - 4 - NS)
                        elif not (first and j < 5):
                            pe.wait_ge(s_yrow, j - 4)
                        stage_d(yy[1 - p], 1 - p, e[j - 3 if tokens else u - 3])

            pe.wait_ge(s_logit, NG)
            e = experts(0, 0, 3)
            for u in range(RING):
                if u == 2:
                    count(1, hT[0])
                    pe.wait_ge(s_cnt_read, NG)
                step(0, u, e, first=True)
            e = experts(1, -3, 3)
            for u in range(RING):
                step(1, u, e, first=True)
            with pe.Fori(2, half) as i:
                e = experts(i, -3, 3)
                for u in range(RING):
                    step(i, u, e)
            pe.wait_ge(s_etile, 2)
            with pe.Fori(half, 2 * half) as i:
                e = experts(i, -3, 3)
                for u in range(RING):
                    step(i, u, e)
            e = {NS + k: v for k, v in experts(2 * half, -3, 0).items()}
            e.update({j: [SHARED] * 2 for j in range(NS, NJ)})
            for j in range(NS, NJ + 3):
                step(j // RING, j % RING, e, last=max(0, j - NJ + 1))

        @block.scalar
        def _(act):
            for i in range(2):
                t = slice(i * GP, (i + 1) * GP)
                act.dma_start(xs[:, t, :], x[:, t, :]).then_inc(s_x[i], 16)
            act.dma_start(gx[:, :], g_both.to_broadcast([P, 2])).then_inc(s_small, 16)
            act.dma_start(gw[:, :], gate_w).then_inc(s_small, 16)
            act.wait_ge(s_const, 3)

            def weights_high(g, it, u):
                n = piece(g, it, u)
                act.wait_ge(s_wst[u // 2], it * 16 + (g * H // RING * 16 + 16))
                act.copy(wH[:, bass.ds(n * WP, WP)], wst[:, u // 2, :]).then_inc(s_wH, 1)

            def q_pair(g, m):
                act.wait_ge(s_tp, g * GP + m + 1)
                for q in range(2):
                    b = 2 * m + q
                    src = tp[m % 2][:, q * L:(q + 1) * L].rearrange("p (c s i) -> p s c i", c=C, i=HALF)
                    dst = qT[:, :, :, :, b * HALF:(b + 1) * HALF].rearrange("p h s c i -> p (h s) c i")
                    mm = act.copy(dst, src)
                mm.then_inc(s_qT, 1)

            def token_stage(m):
                act.wait_ge(s_tp, NG * GP + m + 1)
                if m:
                    act.wait_ge(s_lg, m)
                act.copy(tH[:, 0, :], tp[0][:, :]).then_inc(s_tH, 1)

            def copy_logits(bank, g, m):
                act.wait_ge(s_lg, g * GP + m + 1)
                act.copy(lt[:, m * 2 * P:(m + 1) * 2 * P], bank[0:2 * NR, 0:2 * P]).then_inc(s_lt, 1)

            def scores(g):
                act.wait_ge(s_logit, g + 1)
                if g:
                    act.wait_ge(s_gates, g)
                act.activation(score[:, :, :], logit[:, :, :], ACT.Sigmoid).then_inc(s_score, 1)

            def root(i, mv, tiles=slice(0, GB)):
                act.activation(std[:, i, tiles], mv[:, tiles, 1], ACT.Sqrt, bias=epsc[:, :]).then_inc(s_std, 1)

            def root_pair(g, m):
                act.wait_ge(s_mv[1], g * GB + 2 * m + 2)
                root(1, mv2, slice(2 * m, 2 * m + 2))

            def silu_pair(bank, p, used):
                if used is not None:
                    act.wait_ge(s_hid, used)
                act.activation(silu[:, p, :, :], bank[:, :].rearrange("p (q b n) -> p q b n", q=2, b=2)[:, :, 0, :],
                               ACT.Silu).then_inc(s_silu, 1)

            def high_hidden(bank, p, n, used):
                act.wait_ge(s_hT, n + 1)
                if used is not None:
                    act.wait_ge(s_down, used)
                act.copy(hTH[:, p, :], bank[:, 0:2 * P]).then_inc(s_hTH, 1)

            def clear_slots(g):
                act.dma_start(xg_d[g].rearrange("(p r) d -> p r d", p=P),
                              zero[:, :].unsqueeze(1).to_broadcast([P, NT, L])).then_inc(s_xg_zero[g], 16)

            def scale(g, first, end):
                act.wait_ge(s_gates, g + 1)
                for n in range(first, end):
                    t, k = divmod(n, TOPK)
                    act.activation(sx[:, n, :], xn[:, g * GB + t, :], ACT.Copy,
                                   scale=gates[:, g, k, t:t + 1]).then_inc(s_sx, 1)

            act.activation(unused[:, :], epsc[:, :], ACT.Sqrt, bias=epsc[:, :])
            for i in range(2):
                act.wait_ge(s_mv[0], (i + 1) * GP)
                root(0, mv1, slice(i * GP, (i + 1) * GP))
            act.dma_start(xs[:, GB:, :], x[:, GB:, :]).then_inc(s_x[2], 16)
            for m in range(GP):
                q_pair(0, m)
            act.activation(tg[:, :], gx[:, :], ACT.Tanh).then_inc(s_tg, 1)
            with act.Fori(0, H // RING) as it:
                for u in (0, 2):
                    weights_high(0, it, u)
            act.wait_ge(s_mv[0], NG * GB)
            act.wait_ge(s_z, H + 2)
            root(0, mv1)
            act.wait_ge(s_kt[2], 16)
            clear_slots(0)
            for m in range(GP):
                q_pair(1, m)
                root_pair(0, m)
            for n in range(0, TOK, 2):
                token_stage(n // 2)
                weights_high(1, n // RING, n % RING)
                copy_logits(att[0], 0, n // 2)
            weights_high(1, TOK // RING, 0)
            scores(0)
            weights_high(1, TOK // RING, 2)
            for u in (0, 2):
                weights_high(1, TOK // RING + 1, u)
            act.wait_ge(s_kv, NG * H)
            clear_slots(1)
            scale(0, 0, GB)
            root_pair(1, 0)
            act.wait_ge(s_z, NG * H + 2)
            scale(0, GB, GB * TOPK)
            root_pair(1, 1)
            for j in range(GP):
                act.wait_ge(s_tp, A_SLOT - GP + j + 1)
                if j != 1:
                    act.wait_ge(s_lg, GP + max(0, j - 1))
                act.copy(tH[:, j % 2, :], tp[j % 2][:, :]).then_inc(s_tH, 1)
                if j + 2 < GP:
                    root_pair(1, j + 2)
                if j == 0:
                    act.wait_ge(s_rows, 1)
                else:
                    copy_logits(hT[(j - 1) % 2], 1, j - 1)
            copy_logits(hT[(GP - 1) % 2], 1, GP - 1)
            scores(1)

            def step(i, u, first=False, last=0):
                j, p = i * RING + u, u % 2

                def used(n):
                    return None if first and n <= 0 else n

                for stage in order(j):
                    if stage == "A" and last == 0:
                        act.wait_ge(s_tp, j + (A_SLOT + 1))
                        if first and j < 2:
                            act.wait_ge(s_lg, T_SLOT - 1 + j)
                        else:
                            act.wait_ge(s_up, j - 1)
                        act.copy(tH[:, p, :], tp[p][:, :]).then_inc(s_tH, 1)
                    elif stage == "B" and last <= 1 and not (first and j < 1):
                        act.wait_ge(s_up, j)
                        silu_pair(up[1 - p], 1 - p, used(j - 2))
                    elif stage == "C" and last <= 2 and not (first and j < 2):
                        high_hidden(hT[p], p, j - 2, used(j - 3))
                    elif stage == "D" and not (first and j < 3) and not (isinstance(j, int) and j >= NS + 3):
                        act.wait_ge(s_down, j - 2)
                        r = (u + 1) % RING
                        if not (first and j < 7):
                            act.wait_ge(s_stored[r], i * 16 + (0 if u == RING - 1 else -16))
                        act.copy(yrow[:, r, :, :].rearrange("p t n -> p (t n)"), yy[1 - p][:, :]).then_inc(s_yrow, 1)

            for i in range(2):
                for u in range(RING):
                    step(i, u, first=True)
                    n = (i * RING + u - 2) * 4
                    if 0 <= n < GB * TOPK:
                        act.wait_ge(s_sent[0], 16 * GB * TOPK)
                        scale(1, n, n + 4)
            with act.Fori(2, 2 * half) as i:
                for u in range(RING):
                    step(i, u)
            for j in range(NS, NJ + 3):
                step(j // RING, j % RING, last=max(0, j - NJ + 1))

        @block.vector
        def _(dve):
            chain = [0]

            def linked(ins):
                chain[0] += 1
                ins.then_inc(s_rank, 1)
                dve.wait_ge(s_rank, chain[0])

            def mean_var(i, g, mv):
                for b in range(GB):
                    dve.wait_ge(s_st[i], g * GB + b + 1)
                    dve.bn_aggr(mv[:, b, :], stats[:, i, b, :]).then_inc(s_mv[i], 1)

            def compare(g):
                shape = [P, GB, NR, NR]
                mine, other = (score[:, :, :].unsqueeze(d).to_broadcast(shape) for d in (3, 2))
                gt, eq = (v[:, :, :].rearrange("p (t e) f -> p t e f", e=NR) for v in (cgt, ceq))
                dve.wait_ge(s_score, g + 1)
                dve.tensor_tensor(gt, other, mine, ALU.is_gt)
                linked(dve.tensor_tensor(eq, other, mine, ALU.is_equal))
                flat = ceq[:, :, :].rearrange("p (t e) f -> p t (e f)", e=NR)
                linked(dve.tensor_tensor(flat, flat, earlier[:, :].unsqueeze(1).to_broadcast([P, GB, NR * NR]), ALU.mult))
                linked(dve.tensor_tensor(cgt[:, :, :], cgt[:, :, :], ceq[:, :, :], ALU.add))

            def top_two(g):
                sc = score[:, :, :].rearrange("p t e -> p (t e)")
                linked(dve.tensor_reduce(rank[:, :], cgt[:, :, :], AX.X, ALU.add))
                if g:
                    dve.wait_ge(s_cnt, g)
                dve.tensor_scalar(both[:, :], rank[:, :], float(TOPK), None, ALU.is_lt).then_inc(s_both, 1)
                for k in range(TOPK):
                    ins = dve.tensor_scalar(sel[:, k, :], rank[:, :], float(k), None, ALU.is_equal)
                linked(ins)
                linked(dve.tensor_tensor(pick[:, :, :], sel[:, :, :], sc.unsqueeze(1).to_broadcast([P, TOPK, GB * NR]),
                                         ALU.mult))
                dve.tensor_reduce(gates[:, g, :, :].rearrange("p k t -> p (k t)"),
                                  pick[:, :, :].rearrange("p k (t e) -> p (k t) e", e=NR),
                                  AX.X, ALU.add).then_inc(s_gates, 1)

            def slots(g, bank):
                dve.wait_ge(s_cnt, g + 1)
                dve.tensor_copy(cnt[:, :], bank[:, ROUTE:ROUTE + (GB + 1) * NR]).then_inc(s_cnt_read, 1)
                dve.wait_ge(s_cnt_read, g + 1)
                total = cnt[:, GB * NR:]
                sq = [P, NR, NR]
                wide = cgt[:, 0:NR, :]
                linked(dve.tensor_tensor(wide, total.unsqueeze(2).to_broadcast(sq), thr.unsqueeze(1).to_broadcast(sq),
                                         ALU.is_gt))
                linked(dve.tensor_reduce(ntile[:, :], wide, AX.X, ALU.add))
                linked(dve.tensor_tensor(wide, before.rearrange("p (e f) -> p e f", f=NR),
                                         ntile[:, :].unsqueeze(1).to_broadcast(sq), ALU.mult))
                linked(dve.tensor_reduce(base[:, :], wide, AX.X, ALU.add))
                linked(dve.scalar_tensor_tensor(
                    out=slot[:, :].rearrange("p (t e) -> p t e", e=NR),
                    in0=base[:, :].unsqueeze(1).to_broadcast([P, GB, NR]), scalar=float(P),
                    in1=cnt[:, 0:GB * NR].rearrange("p (t e) -> p t e", e=NR), op0=ALU.mult, op1=ALU.add))
                linked(dve.tensor_tensor(pick[:, :, :], sel[:, :, :],
                                         slot[:, :].unsqueeze(1).to_broadcast([P, TOPK, GB * NR]), ALU.mult))
                linked(dve.tensor_reduce(slotf[:, :], pick[:, :, :].rearrange("p k (t e) -> p (k t) e", e=NR),
                                         AX.X, ALU.add))
                dve.tensor_copy(idx[:, g, :, :].rearrange("p k t -> p (k t)"), slotf[:, :]).then_inc(s_idx, 1)

            def slot_experts(g):
                linked(dve.tensor_tensor(ends[:, :], base[:, :], ntile[:, :], ALU.add))
                tall = cgt[:, 0:NT, :]
                shape = [P, NT, NR]
                linked(dve.tensor_tensor(tall, tile_no.unsqueeze(2).to_broadcast(shape),
                                         ends[:, :].unsqueeze(1).to_broadcast(shape), ALU.is_ge))
                linked(dve.tensor_reduce(etf[:, :], tall, AX.X, ALU.add))
                dve.tensor_scalar(etile[:, g, :], etf[:, :], float(NR - 1), float(WE), ALU.min, ALU.mult).then_inc(s_etile, 1)

            def low_tokens(bank, p, n):
                dve.wait_ge(s_tH, n + 1)
                dve.tensor_tensor(tL[:, p, :], bank[:, :], tH[:, p, :].bitcast(F32), ALU.subtract).then_inc(s_tL, 1)

            def hidden(bank, p, n):
                dve.wait_ge(s_silu, n + 1)
                dve.tensor_tensor(hid[:, p, :, :], bank[:, :].rearrange("p (q b n) -> p q b n", q=2, b=2)[:, :, 1, :],
                                  silu[:, p, :, :], ALU.mult).then_inc(s_hid, 1)

            def low_hidden(bank, p, n):
                dve.wait_ge(s_hTH, n + 1)
                dve.tensor_tensor(hTL[:, p, :], bank[:, 0:2 * P], hTH[:, p, :].bitcast(F32),
                                  ALU.subtract).then_inc(s_hTL, 1)

            def shared(bank, t):
                xp = xs[:, bass.ds(t, 2), :].rearrange("p t n -> p (t n)")
                dve.scalar_tensor_tensor(out=xp, in0=bank[:, :], scalar=tg[:, 1:2], in1=xp,
                                         op0=ALU.mult, op1=ALU.add).then_inc(s_shared, 1)

            def norm_q(g, b):
                if b >= 4:
                    dve.wait_ge(s_tp, g * GP + b // 2 - 1)
                dve.tensor_scalar(xq[:, b % 4, :], xs[:, g * GB + b, :], mv1[:, b, 0:1], rstd[:, 0, b:b + 1],
                                  ALU.subtract, ALU.mult).then_inc(s_xq, 1)

            def norm_pair(g, m):
                for b in (2 * m, 2 * m + 1):
                    dve.tensor_scalar(xn[:, g * GB + b, :], xs[:, g * GB + b, :], mv2[:, b, 0:1], rstd[:, 1, b:b + 1],
                                      ALU.subtract, ALU.mult).then_inc(s_xn, 1)

            def attended(g, m):
                j = g * GP + m
                xp = xs[:, 2 * j:2 * j + 2, :].rearrange("p t n -> p (t n)")
                dve.wait_ge(s_isum, j + 1)
                dve.scalar_tensor_tensor(out=xp, in0=att[m % 2][:, :], scalar=tg[:, 0:1], in1=xp,
                                         op0=ALU.mult, op1=ALU.add).then_inc(s_attended, 1)

            def statistics(g, m):
                dve.wait_ge(s_attended, g * GP + m + 1)
                for b in (2 * m, 2 * m + 1):
                    dve.bn_stats(stats[:, 1, b, :], xs[:, g * GB + b, :]).then_inc(s_st[1], 1)
                for b in (2 * m, 2 * m + 1):
                    dve.wait_ge(s_st[1], g * GB + b + 1)
                    dve.bn_aggr(mv2[:, b, :], stats[:, 1, b, :]).then_inc(s_mv[1], 1)

            def inverse(g, m):
                dve.wait_ge(s_std, 3 + g * GP + m + 1)
                linked(dve.reciprocal(rstd[:, 1, 2 * m:2 * m + 2], std[:, 1, 2 * m:2 * m + 2]))

            def head(g, it, u):
                h = it * RING + u
                yd = yD[u % 2][:, 0:DCOLS].rearrange("p (s n j) -> p s n j", s=2, j=HALF)
                yo = yO[u % 2][:, 0:OCOLS].rearrange("p (n j) -> p n j", j=HALF)
                q_h = qT[:, bass.ds(h, 1), :, :, :].rearrange("p h s c n -> p s (h c n)")
                zh = z[:, :, :, bass.ds(h * HD, HD)]
                ni = CB * HALF
                dve.wait_ge(s_conv, h + (g * H + 1 + RING))
                dve.tensor_tensor(zh[:, 0, :, :].rearrange("p n (s j) -> p s n j", s=2), yd,
                                  q_h.unsqueeze(3).to_broadcast([P, 2, ni, HALF]), ALU.mult)
                dve.tensor_tensor(zh[:, 1, :, HALF:], yo,
                                  q_h[:, 0, :].unsqueeze(2).to_broadcast([P, ni, HALF]), ALU.mult)
                q_j = q_h[:, 1, :].rearrange("p (n j) -> p n j", j=HALF)
                dve.tensor_tensor(zh[:, 1, :, 0:HALF].rearrange("p (n j) i -> p n i j", j=HALF),
                                  yo.rearrange("p (n i) j -> p n i j", i=HALF),
                                  q_j.unsqueeze(2).to_broadcast([P, CB, HALF, HALF]),
                                  ALU.mult).then_inc(s_z, 1)

            def weights_low(g, it, u):
                if u % 2 == 0:
                    n = piece(g, it, u)
                    dve.wait_ge(s_wH, n + 1)
                    dve.tensor_tensor(wL[:, bass.ds(n * WP, WP)], wst[:, u // 2, :],
                                      wH[:, bass.ds(n * WP, WP)].bitcast(F32), ALU.subtract).then_inc(s_wL, 1)

            def add_logits(bank):
                dve.tensor_reduce(logit[:, :, :],
                                  bank[:, ROUTE:ROUTE + GB * 2 * NR].rearrange("p (t v e) -> p t e v", v=2, e=NR),
                                  AX.X, ALU.add).then_inc(s_logit, 1)

            def token_stage(m):
                if m:
                    dve.wait_ge(s_lg, m)
                low_tokens(tp[0], 0, m)

            dve.sem_inc(s_z, 2)
            dve.sem_inc(s_wL, 2)
            dve.wait_ge(s_kp, 32)
            dve.tensor_tensor(kp[:, P - 1:P], kp[:, P - 1:P], dsk[:, :], ALU.add).then_inc(s_kpd, 1)
            for i in range(3):
                if i < 2:
                    dve.wait_ge(s_x[i], 16)
                    for b in range(i * GP, (i + 1) * GP):
                        dve.bn_stats(stats[:, 0, b, :], xs[:, b, :]).then_inc(s_st[0], 1)
                    for b in range(i * GP, (i + 1) * GP):
                        dve.wait_ge(s_st[0], b + 1)
                        dve.bn_aggr(mv1[:, b, :], stats[:, 0, b, :]).then_inc(s_mv[0], 1)
                if i:
                    half_group = slice((i - 1) * GP, i * GP)
                    dve.wait_ge(s_std, i)
                    linked(dve.reciprocal(rstd[:, 0, half_group], std[:, 0, half_group]))
                    for b in range((i - 1) * GP, i * GP):
                        norm_q(0, b)
            dve.wait_ge(s_small, 48)
            dve.tensor_copy(upper[:, :], const[:, K_UP:K_UP + P]).then_inc(s_upper, 1)
            linked(dve.tensor_copy(earlier[:, :], before))
            gw3 = gw[:, :].rearrange("p (c e) -> p c e", e=NR)
            linked(dve.tensor_copy(gwHL[:, :, 0, :], gw3))
            dve.tensor_tensor(gwHL[:, :, 1, :], gw3, gwHL[:, :, 0, :].bitcast(F32), ALU.subtract).then_inc(s_gw, 2)
            dve.wait_ge(s_qT, GP)
            dve.wait_ge(s_mv[0], GB)
            dve.wait_ge(s_x[2], 16)
            with dve.Fori(0, H // RING) as it:
                for u in range(RING):
                    head(0, it, u)
                    weights_low(0, it, u)
                    if u % 2:
                        b = it * 2 + u // 2
                        dve.bn_stats(stats[:, 0, b, :], xs[:, b + GB, :]).then_inc(s_st[0], 1)
            dve.wait_ge(s_xq, GB)
            mean_var(0, 1, mv1)
            dve.wait_ge(s_std, 3)
            linked(dve.reciprocal(rstd[:, 0, :], std[:, 0, :]))
            dve.wait_ge(s_tg, 1)
            for m in range(GP):
                norm_q(1, 2 * m)
                norm_q(1, 2 * m + 1)
                attended(0, m)
                statistics(0, m)
                if m:
                    inverse(0, m - 1)
                    norm_pair(0, m - 1)
            inverse(0, GP - 1)
            norm_pair(0, GP - 1)
            dve.wait_ge(s_isum, GP)
            dve.wait_ge(s_qT, NG * GP)
            for n in range(TOK):
                head(1, n // RING, n % RING)
                if n % 2 == 0:
                    token_stage(n // 2)
                weights_low(1, n // RING, n % RING)
            for n in range(TOK, H):
                head(1, n // RING, n % RING)
                weights_low(1, n // RING, n % RING)
                if n == TOK:
                    dve.wait_ge(s_rows, 1)
                    add_logits(att[0])
                elif n == TOK + 1:
                    dve.wait_ge(s_tp, NG * GP)
                    compare(0)
                elif n == TOK + 3:
                    top_two(0)
            slots(0, tp[0])
            dve.wait_ge(s_xn, GB)

            def residual(m):
                attended(1, m)
                statistics(1, m)

            def normalised(m):
                inverse(1, m)
                norm_pair(1, m)

            def low(j):
                if j != 1:
                    dve.wait_ge(s_lg, GP + max(0, j - 1))
                low_tokens(tp[j % 2], j % 2, GP + j)

            residual(0)
            slot_experts(0)
            residual(1)
            normalised(0)
            residual(2)
            normalised(1)
            low(0)
            normalised(2)
            residual(3)
            low(1)
            normalised(3)
            low(2)
            low(3)
            dve.wait_ge(s_rows, NG)
            dve.wait_ge(s_score, 1)
            add_logits(hT[0])

            def step(i, u, first=False, last=0):
                j, p = i * RING + u, u % 2

                for stage in order(j):
                    if stage == "A" and last == 0:
                        if first and j < 2:
                            dve.wait_ge(s_lg, T_SLOT - 1 + j)
                        else:
                            dve.wait_ge(s_up, j - 1)
                        low_tokens(tp[p], p, j + T_SLOT)
                    elif stage == "B" and last <= 1 and not (first and j < 1):
                        if first and j == 1:
                            top_two(1)
                        if not (first and j < 3):
                            dve.wait_ge(s_hT, j - 2)
                        hidden(up[1 - p], 1 - p, j - 1)
                    elif stage == "C" and last <= 2 and not (first and j < 2):
                        if not (first and j < 4):
                            dve.wait_ge(s_down, j - 3)
                        low_hidden(hT[p], p, j - 2)
                    elif stage == "D" and isinstance(j, int) and j >= NS + 3:
                        dve.wait_ge(s_down, j - 2)
                        shared(yy[1 - p], 2 * (j - 3 - NS))

            def finish(t):
                dve.wait_ge(s_got[t], 16 * TOPK)
                dve.tensor_tensor(got[:, t, 0, :], got[:, t, 0, :], got[:, t, 1, :], ALU.add).then_inc(s_sum, 1)
                dve.wait_ge(s_sum, t + 1)
                dve.scalar_tensor_tensor(out=xs[:, t, :], in0=got[:, t, 0, :], scalar=tg[:, 1:2], in1=xs[:, t, :],
                                         op0=ALU.mult, op1=ALU.add).then_inc(s_fin, 1)

            for u in range(RING):
                if u == 0:
                    compare(1)
                step(0, u, first=True)
                if u == 1:
                    slots(1, hT[0])
                    slot_experts(1)
            with dve.Fori(1, 2 * half - 1) as i:
                for u in range(RING):
                    step(i, u)
            fin = 0
            for j in range(NS - RING, NJ + 3):
                if j >= NS + 3:
                    dve.wait_ge(s_fin, fin)
                step(j // RING, j % RING, last=max(0, j - NJ + 1))
                if j >= NS + 3:
                    dve.wait_ge(s_shared, j - 2 - NS)
                end = min(GB, j + 1 - NS + RING) if j < NS + 5 else GB + 1 + 3 * (j - NS - 5) // 2
                for t in range(fin, end):
                    finish(t)
                fin = end


def constants(np):
    k = np.zeros((P, NK), np.float32)
    k[:, K_ID:K_ID + P] = np.eye(P)
    k[:, K_UP:K_UP + P] = np.triu(np.ones((P, P)), 1)
    k[:, K_BEF:K_BEF + NR * NR] = np.tril(np.ones((NR, NR)), -1).reshape(-1)
    k[:, K_THR:K_THR + NR] = P * np.arange(NR)
    k[:, K_TILE:K_TILE + NT] = np.arange(NT)
    return k


def kernel(x, ctx_2048, g_xattn, g_ffn, L0_xattn_ssm_kernel, L0_xattn_D, L0_ffn_gate_w,
           L0_ffn_w1, L0_ffn_w2, L0_ffn_w3, L0_ffn_ws1, L0_ffn_ws2, L0_ffn_ws3):
    import numpy as np
    import concourse.bacc as bacc
    from concourse.bass_utils import run_bass_kernel_spmd as run

    cont = np.ascontiguousarray
    a = [np.asarray(v) for v in (x, ctx_2048, g_xattn, g_ffn, L0_xattn_ssm_kernel, L0_xattn_D, L0_ffn_gate_w,
                                 L0_ffn_w1, L0_ffn_w2, L0_ffn_w3, L0_ffn_ws1, L0_ffn_ws2, L0_ffn_ws3)]
    x, cx, gxa, gff, ssm, dsk, gate, w1, w2, w3, ws1, ws2, ws3 = a
    kt = cx.reshape(NG, GB, H, 2, HALF, C, P)[..., ::-1].transpose(6, 0, 2, 3, 5, 1, 4)
    kpad = np.zeros((H, KPAD), ssm.dtype)
    kpad[:, P - 1:] = ssm
    up = np.stack([np.concatenate([ws1[None], w1]), np.concatenate([ws3[None], w3])], 1)
    up = up.reshape(NE, 2, HID, C, P).transpose(4, 0, 3, 1, 2).reshape(P, NE, C * 2 * HID)
    down = np.concatenate([ws2[None], w2]).transpose(2, 0, 1)
    w_all = np.concatenate([up, down], 2)
    arrays = {
        "x": cont(x.transpose(1, 0, 2)),
        "kt": cont(kt).reshape(P, NG, H * 2 * CB * HALF),
        "kpad": kpad,
        "d_skip": cont(dsk.reshape(H, 1)),
        "g_both": cont(np.concatenate([gxa, gff]).reshape(1, 2)),
        "gate_w": cont(gate.reshape(NR, C, P).transpose(2, 1, 0)).reshape(P, C * NR),
        "w_all": cont(w_all).reshape(P, NPIECE, WP),
        "consts": constants(np),
    }
    nc = bacc.Bacc("TRN2", target_bir_lowering=False, num_devices=1)
    ins = [nc.dram_tensor(f"in_{n}", v.shape, F32, kind="ExternalInput").ap() for n, v in arrays.items()]
    xg_d = [nc.dram_tensor(f"xg_d{g}", (NT * P, L), F32, kind="Internal").ap() for g in range(NG)]
    y_d = [nc.dram_tensor(f"y_d{g}", (NT * P, L), F32, kind="Internal").ap() for g in range(NG)]
    kpad_d = nc.dram_tensor("kpad_d", (H, KPAD), F32, kind="Internal").ap()
    out = nc.dram_tensor("out", (P, B, L), F32, kind="ExternalOutput").ap()
    build(nc, *ins, kpad_d, xg_d, y_d, out)
    r = run(nc, [{f"in_{n}": v for n, v in arrays.items()}], core_ids=[0])
    return cont(r.results[0]["out"].transpose(1, 0, 2))
```
